# Optimizing a Trainium2 kernel written in Bass

```python
import numpy as np
import jax
import jax.numpy as jnp

def _softmax(x, axis=-1):
    return jax.nn.softmax(x, axis=axis)

def _gelu(x):
    return jax.nn.gelu(x, approximate=True)

def _silu(x):
    return jax.nn.silu(x)

def _sigmoid(x):
    return jax.nn.sigmoid(x)

def _layernorm(x, axis=-1, eps=1e-05):
    m = jnp.mean(x, axis=axis, keepdims=True)
    v = jnp.var(x, axis=axis, keepdims=True)
    return (x - m) / jnp.sqrt(v + eps)

def _scatter_add(tgt, idx, src, axis=0):
    return tgt.at[idx].add(src)

def _segment_sum(src, seg, n):
    return jax.ops.segment_sum(src, seg, n)
kernel_name = 'mk_gnn_resnorm_d2_gnn_r64_eb349b'

def setup_inputs(seed: int=0):
    np.random.seed(seed)
    _w = jnp.asarray

    def _rec_inputs():
        import jax
        import jax.numpy as jnp
        _gk = jax.random.key(seed)
        x = -0.0003713 + 1 * jax.random.normal(jax.random.fold_in(_gk, 1), (50000, 256), jnp.float32)
        src = jax.random.randint(jax.random.fold_in(_gk, 2), (12500,), 0, 50000, jnp.int32)
        dst = jnp.minimum((50000 * jax.random.uniform(jax.random.fold_in(_gk, 3), (12500,)) ** 2.0).astype(jnp.int32), 49999)
        _o = jnp.argsort(dst, stable=True)
        src = src[_o]
        dst = dst[_o]
        edge_attr_64 = -8.4373e-05 + 1.00001 * jax.random.normal(jax.random.fold_in(_gk, 12), (12500, 64), jnp.float32)
        edge_weight = jax.random.uniform(jax.random.fold_in(_gk, 14), (12500,), jnp.float32, 0.0, 0.999998)
        node_type_100 = jax.random.randint(jax.random.fold_in(_gk, 15), (50000,), 0, 100, jnp.int32)
        return (x, src, dst, edge_attr_64, edge_weight, node_type_100)
    x, src, dst, edge_attr_64, edge_weight, node_type_100 = _rec_inputs()

    def _L0_gnn_setup():
        import jax, jax.numpy as jnp
        import numpy as np
        N = 50000
        M = 12500
        H = 8
        DK = 32
        DV = 32
        DE = 256
        INV_SQRT_DK = float(1.0 / np.sqrt(DK))
        key = jax.random.key(seed)
        k0, k1, k2, k3 = jax.random.split(key, 4)
        x = jax.random.normal(k0, (N, DE), dtype=jnp.float32)
        edge_index = jax.random.randint(k1, (2, M), 0, N, dtype=jnp.int64)
        qkv_out = (2 * DK + DV) * H
        W_qkv = jax.random.normal(k2, (qkv_out, DE), dtype=jnp.float32) / np.sqrt(DE).astype(np.float32)
        b_qkv = jnp.zeros((qkv_out,), dtype=jnp.float32)
        W_ff = jax.random.normal(k3, (DE, DV * H), dtype=jnp.float32) / np.sqrt(DV * H).astype(np.float32)
        b_ff = jnp.zeros((DE,), dtype=jnp.float32)
        return {'x': x, 'edge_index': edge_index, 'W_qkv': W_qkv, 'b_qkv': b_qkv, 'W_ff': W_ff, 'b_ff': b_ff}
    _L0_gnn_all = _L0_gnn_setup()
    _L0_gnn_in = {k: v for k, v in _L0_gnn_all.items() if k in ('W_qkv', 'b_qkv', 'W_ff', 'b_ff')}
    del _L0_gnn_all

    def _L1_gnn_setup():
        import jax, jax.numpy as jnp
        import numpy as np
        N = 50000
        E = 12500
        C = 256
        RBF = 64
        NUM_SPECIES = 100
        CUTOFF = 5.0
        key = jax.random.key(seed)
        ks = jax.random.split(key, 10)
        node_z = jax.random.randint(ks[0], (N,), 0, NUM_SPECIES)
        node_feats = jax.random.normal(ks[1], (N, C), dtype=jnp.float32)
        senders = jax.random.randint(ks[2], (E,), 0, N)
        receivers = jnp.sort(jax.random.randint(ks[3], (E,), 0, N))
        edge_weight = jax.random.uniform(ks[4], (E,), dtype=jnp.float32)
        edge_feats = jax.random.normal(ks[5], (E, RBF), dtype=jnp.float32)
        embed_table = jax.random.normal(ks[6], (NUM_SPECIES, C), dtype=jnp.float32)
        lim_dp = float(np.sqrt(6.0 / (RBF + C)))
        W_dist = jax.random.uniform(ks[7], (RBF, C), minval=-lim_dp, maxval=lim_dp, dtype=jnp.float32)
        b_dist = jnp.zeros((C,), dtype=jnp.float32)
        lim_cb = float(np.sqrt(6.0 / (2 * C + C)))
        W_comb = jax.random.uniform(ks[8], (2 * C, C), minval=-lim_cb, maxval=lim_cb, dtype=jnp.float32)
        b_comb = jnp.zeros((C,), dtype=jnp.float32)
        return {'node_z': node_z, 'node_feats': node_feats, 'senders': senders, 'receivers': receivers, 'edge_weight': edge_weight, 'edge_feats': edge_feats, 'embed_table': embed_table, 'W_dist': W_dist, 'b_dist': b_dist, 'W_comb': W_comb, 'b_comb': b_comb}
    _L1_gnn_all = _L1_gnn_setup()
    _L1_gnn_in = {k: v for k, v in _L1_gnn_all.items() if k in ('embed_table', 'W_dist', 'b_dist', 'W_comb', 'b_comb')}
    del _L1_gnn_all
    return {'x': x, 'src': src, 'dst': dst, 'edge_attr_64': edge_attr_64, 'edge_weight': edge_weight, 'node_type_100': node_type_100, 'L0_gnn_W_qkv': _L0_gnn_in['W_qkv'], 'L0_gnn_b_qkv': _L0_gnn_in['b_qkv'], 'L0_gnn_W_ff': _L0_gnn_in['W_ff'], 'L0_gnn_b_ff': _L0_gnn_in['b_ff'], 'L1_gnn_embed_table': _L1_gnn_in['embed_table'], 'L1_gnn_W_dist': _L1_gnn_in['W_dist'], 'L1_gnn_b_dist': _L1_gnn_in['b_dist'], 'L1_gnn_W_comb': _L1_gnn_in['W_comb'], 'L1_gnn_b_comb': _L1_gnn_in['b_comb']}

def reference(x, src, dst, edge_attr_64, edge_weight, node_type_100, L0_gnn_W_qkv, L0_gnn_b_qkv, L0_gnn_W_ff, L0_gnn_b_ff, L1_gnn_embed_table, L1_gnn_W_dist, L1_gnn_b_dist, L1_gnn_W_comb, L1_gnn_b_comb):
    import jax
    import jax.numpy as jnp

    def _L0_gnn_ref(x, edge_index, W_qkv, b_qkv, W_ff, b_ff):
        import jax, jax.numpy as jnp
        import numpy as np
        N = 50000
        M = 12500
        H = 8
        DK = 32
        DV = 32
        DE = 256
        INV_SQRT_DK = float(1.0 / np.sqrt(DK))
        senders, receivers = (edge_index[0], edge_index[1])
        qkv = x @ W_qkv.T + b_qkv
        Q = qkv[:, :DK * H].reshape(N, H, DK)
        K = qkv[:, DK * H:2 * DK * H].reshape(N, H, DK)
        V = qkv[:, 2 * DK * H:].reshape(N, H, DV)
        att = jnp.einsum('mhd,mhd->mh', Q[receivers], K[senders]) * INV_SQRT_DK
        seg_max = jax.ops.segment_max(att, receivers, num_segments=N)
        e = jnp.exp(att - jax.lax.stop_gradient(seg_max)[receivers])
        denom = jax.ops.segment_sum(e, receivers, num_segments=N)[receivers]
        attention = jnp.where(denom > 0, e / denom, jnp.zeros_like(e))
        out = jax.ops.segment_sum(attention[:, :, None] * V[senders], receivers, num_segments=N)
        return out.reshape(N, H * DV) @ W_ff.T + b_ff

    def _L1_gnn_ref(node_z, node_feats, senders, receivers, edge_weight, edge_feats, embed_table, W_dist, b_dist, W_comb, b_comb):
        import jax, jax.numpy as jnp
        import numpy as np
        N = 50000
        E = 12500
        C = 256
        RBF = 64
        NUM_SPECIES = 100
        CUTOFF = 5.0
        cut = 0.5 * (jnp.cos(edge_weight * jnp.pi / CUTOFF) + 1.0)
        cut = cut * (edge_weight < CUTOFF).astype(jnp.float32)
        W = (edge_feats @ W_dist + b_dist) * cut[:, None]
        x_j = embed_table[node_z][senders]
        msgs = x_j * W
        agg = jax.ops.segment_sum(msgs, receivers, num_segments=node_feats.shape[0])
        out = jnp.concatenate([node_feats, agg], axis=1) @ W_comb + b_comb
        return out
    edge_index = jnp.stack([src, dst])
    x = _layernorm(x + _L0_gnn_ref(x, edge_index, L0_gnn_W_qkv, L0_gnn_b_qkv, L0_gnn_W_ff, L0_gnn_b_ff), axis=-1)
    x = _layernorm(x + _L1_gnn_ref(node_type_100, x, src, dst, edge_weight, edge_attr_64, L1_gnn_embed_table, L1_gnn_W_dist, L1_gnn_b_dist, L1_gnn_W_comb, L1_gnn_b_comb), axis=-1)
    return x

_drawn_inputs = setup_inputs


def setup_inputs(seed=0):
    import zlib

    import numpy as np

    out = dict(_drawn_inputs(seed))
    spreads = {'L0_gnn_b_qkv': (0.0, 0.296),
     'L0_gnn_b_ff': (0.0, 0.1),
     'L1_gnn_b_dist': (0.0, 0.324),
     'L1_gnn_b_comb': (0.0, 0.1)}
    factors = {'edge_weight': 8.0}
    for name, (base, spread) in spreads.items():
        noise = np.random.default_rng([zlib.crc32(name.encode()), seed]).standard_normal(out[name].shape)
        drawn = base * np.exp(spread * noise) if base else spread * noise
        out[name] = jnp.asarray(drawn.astype(out[name].dtype))
    for name, factor in factors.items():
        out[name] = (out[name] * factor).astype(out[name].dtype)
    return out
```

```python
from contextlib import ExitStack

import concourse.bass as bass
from concourse import mybir
import numpy as np

P = 128
ALU = mybir.AluOpType
ACT = mybir.ActivationFunctionType
AX = mybir.AxisListType
F32 = mybir.dt.float32
BF16 = mybir.dt.bfloat16
I32 = mybir.dt.int32

EPS = 1e-5
FAR = 1.0e30
SKIP = float(1 << 20)
CUTOFF = 5.0


def after(eng, sem, count):
    if not (isinstance(count, int) and count < 1):
        eng.wait_ge(sem, count)


def back(h, par, k):
    return h + (par - k) // 2, (par - k) % 2


def build(nc, x, src, dst, attr, weight, ntype, w_qkv, b_qkv, w_ff, b_ff, table, w_dist, b_dist, w_comb, b_comb, out):
    N, D = x.shape
    E, RBF = attr.shape
    SPECIES = table.shape[0]
    DC = D // P
    HD = 32
    HPC = P // HD
    SCALE = float(1.0 / np.sqrt(HD))
    ROWS = 4
    STEP = P * ROWS
    G = -(-N // STEP)
    REST = N - (G - 1) * STEP
    REST_J = 3
    REST_P = REST // REST_J
    assert REST_P * REST_J == REST and REST_P % 16 == 0 and REST_P <= P and G % 2 == 0
    EB = 2 * P
    B = -(-E // EB)
    T = 2 * B
    FULL_T, REST_E = divmod(E, P)
    assert T == FULL_T + 1 and B % 2 == 1 and T <= P

    ctx = ExitStack()

    def sb(name, shape, dt=F32):
        return ctx.enter_context(nc.sbuf_tensor(name, shape, dt))

    def sem(name):
        return ctx.enter_context(nc.semaphore(name))

    def sems(name):
        return [sem(f"{name}{i}") for i in range(2)]

    ps = ctx.enter_context(nc.psum_tensor("ps", [P, 8, 512], F32))

    def bank(k):
        return ps[:, k, :].rearrange("p (c n) -> p c n", c=2)

    ident = sb("ident", [P, P])
    ones_mean = sb("ones_mean", [P, P])
    head_sum = sb("head_sum", [P, P])
    lane = sb("lane", [P, 1])
    lane_i = sb("lane_i", [P, 1], I32)
    half_pi = sb("half_pi", [P, 1])
    neg_half = sb("neg_half", [P, ROWS])
    wc = sb("wc", [P, 2 * DC, D])
    wc_mean = sb("wc_mean", [P, 2 * DC])
    w_mix = sb("w_mix", [P, DC, D])
    bc = sb("bc", [P, D])
    bc_mean = sb("bc_mean", [P, 1])
    bff_row = sb("bff_row", [P, D])
    bff_col = sb("bff_col", [P, DC])
    bqkv = sb("bqkv", [P, 3 * DC])
    w_raw = sb("w_raw", [P, 3 * DC + DC, D])
    wT = sb("wT", [P, DC, 4 * D])
    wd = sb("wd", [RBF + 1, D])
    tab = sb("tab", [SPECIES, D])
    tab_res = sb("tab_res", [SPECIES, D])
    tab3 = sb("tab3", [SPECIES, 3, D], BF16)
    rows_i = sb("rows_i", [T, 3, P], I32)
    rows_f = sb("rows_f", [T, 4, P])
    cols = sb("cols", [P, 4, T])
    ct = sb("ct", [P, 4, T])
    ct_i = sb("ct_i", [P, T], I32)
    idx = sb("idx", [P, B, 6], I32)
    fcol = sb("fcol", [P, B, 4])

    xin = sb("xin", [P, 2, ROWS * D])
    zin = sb("zin", [P, 2, ROWS * D])
    zT = sb("zT", [P, 2, DC, ROWS * P])
    stat = sb("stat", [P, 2, ROWS, 6])
    mv = sb("mv", [P, 2, ROWS, 2])
    r1a = sb("r1a", [P, 2, ROWS])
    r1 = sb("r1", [P, 2, ROWS])
    yn = sb("yn", [P, 2, ROWS * D])
    junk = sb("junk", [P, ROWS, D])
    ss = sb("ss", [P, 2, ROWS])
    r2a = sb("r2a", [P, 2, ROWS])
    r2 = sb("r2", [P, 2, ROWS])
    on = sb("on", [P, 2, ROWS * D])

    idx_b = sb("idx_b", [P, 3, 6], I32)
    fcol_b = sb("fcol_b", [P, 2, 4])
    xs = sb("xs", [P, 2, 2, D])
    xd = sb("xd", [P, 2, 2, D])
    ty = sb("ty", [P, 2, 2], I32)
    ty_f = sb("ty_f", [P, 2, 2])
    at = sb("at", [P, 2, 2, RBF])
    atc = sb("atc", [P, 2, RBF + 1])
    dbc = sb("dbc", [P, 2, EB + 1])
    same = sb("same", [P, 2, EB])
    neg = sb("neg", [P, 2, EB])
    hot = sb("hot", [P, EB], BF16)
    xsT = sb("xsT", [P, 2, EB])
    xdT = sb("xdT", [P, 2, 2, EB])
    qT = sb("qT", [P, 2, EB])
    vT = sb("vT", [P, 2, EB])
    prod = sb("prod", [P, 2, EB])
    atT = sb("atT", [RBF + 1, EB])
    emb = sb("emb", [P, 2, EB])
    msg = sb("msg", [P, 2, EB])
    mx = sb("mx", [P, 2, 2, EB + 1])
    dlt = sb("dlt", [P, 2, EB])
    ua = sb("ua", [P, 2, EB])
    ub = sb("ub", [P, 2, EB])
    resc = sb("resc", [P, 2, EB])
    ex = sb("ex", [P, 2, EB])
    ev = sb("ev", [P, 2, EB])
    den = sb("den", [P, 2, 2, EB])
    num = sb("num", [P, 2, 2, EB])
    agg = sb("agg", [P, 2, 2, EB])
    rd = sb("rd", [P, 2, 2, HPC])
    rdx = sb("rdx", [P, 2, 2, P])
    oT = sb("oT", [P, 2, EB])
    zeT = sb("zeT", [P, 2, EB])
    est = sb("est", [P, 2, 6])
    emv = sb("emv", [P, 2, 2])
    er1a = sb("er1a", [P, 2])
    er1 = sb("er1", [P, 2])
    t2 = sb("t2", [P, 2, D])
    ye = sb("ye", [P, 2, 2, D])
    ess = sb("ess", [P, 2])
    er2a = sb("er2a", [P, 2])
    er2 = sb("er2", [P, 2])
    oe = sb("oe", [P, 2, 2, D])

    s_w = sem("weights_landed")
    s_rows = sem("edge_rows_landed")
    s_pad = sem("pads_set")
    s_const = sem("constants_set")
    s_lane = sem("lane_ready")
    s_id = sem("ident_ready")
    s_wchain = sem("weight_arithmetic")
    s_cm = sem("column_mean_ready")
    s_wready = sem("mix_weights_ready")
    s_wtp = sem("weight_transposed")
    s_wtc = sem("weight_copied")
    s_ef = sem("edge_rows_float")
    s_ep = sem("edge_columns_transposed")
    s_ec = sem("edge_columns_copied")
    s_sin = sem("cosine_ready")
    s_echain = sem("edge_arithmetic")
    s_idx = sem("edge_indices_ready")
    s_hs = sem("constants_cleared")
    s_wsum = sem("weight_sums")
    s_tab = sem("table_parts")
    s_pool_passed = sem("pool_waits_passed")
    s_dve_passed = sem("vector_waits_passed")
    n_x = sems("node_rows_landed")
    n_out = sems("node_rows_stored")
    n_z = sem("node_z_ready")
    n_tp = sem("node_z_transposed")
    n_tc = sem("node_zT_copied")
    n_y = sem("node_product_ready")
    n_st = sem("node_stats")
    n_mv = sem("node_moments")
    n_ra = sem("node_var_eps")
    n_r1 = sem("node_rstd1")
    n_yy = sem("node_y_ready")
    n_ss = sem("node_squares_summed")
    n_rb = sem("node_var2_eps")
    n_r2 = sem("node_rstd2")
    n_o = sem("node_output_ready")
    e_at = sems("attributes_landed")
    e_g = sems("gathers_landed")
    e_sc = sems("scatter_landed")
    s_w1 = sem("node_weights_landed")
    e_sci = sem("scatter_indices_copied")
    e_idx = sem("block_indices_copied")
    e_fc = sem("block_columns_copied")
    e_ty = sem("types_float")
    e_atc = sem("attributes_scaled")
    e_bcp = sem("receivers_types_broadcast")
    e_dbc = sem("receivers_copied")
    e_hot = sem("onehot_ready")
    e_same = sem("same_receiver_ready")
    e_neg = sem("restart_offset_ready")
    e_xsp = sem("source_rows_transposed")
    e_xdp = sem("receiver_rows_transposed")
    e_xsc = sem("source_rows_copied")
    e_xdc = sem("receiver_rows_copied")
    e_qp = sem("q_product")
    e_kp = sem("k_product")
    e_vp = sem("v_product")
    e_q = sem("q_ready")
    e_v = sem("v_ready")
    e_prod = sem("qk_ready")
    e_attp = sem("scores_ready")
    e_atp = sem("attributes_transposed")
    e_atT = sem("attributes_copied")
    e_embp = sem("embedding_product")
    e_emb = sem("embedding_copied")
    e_wdp = sem("filter_product")
    e_msg = sem("messages_ready")
    e_m0 = sem("maximum_carried")
    e_m = sem("running_maximum_ready")
    e_d = sem("score_minus_maximum")
    e_ua = sem("maximum_before")
    e_u = sem("maximum_drop")
    e_resc = sem("rescale_ready")
    e_ex = sem("exponential_ready")
    e_ev = sem("weighted_values_ready")
    e_den = sem("denominator_ready")
    e_num = sem("numerator_ready")
    e_agg = sem("aggregate_ready")
    e_denp = sem("denominator_columns")
    e_rd = sem("reciprocal_ready")
    e_rdx = sem("reciprocal_spread")
    e_rdp = sem("reciprocal_broadcast")
    e_o = sem("attention_ready")
    e_ffp = sem("ff_product")
    e_z = sem("edge_z_ready")
    e_zp = sem("edge_z_transposed")
    e_st = sem("edge_stats")
    e_mv = sem("edge_moments")
    e_ra = sem("edge_var_eps")
    e_r1 = sem("edge_rstd1")
    e_aggp = sem("aggregate_product")
    e_t2 = sem("aggregate_term_ready")
    e_mixp = sem("mix_product")
    e_y = sem("edge_y_ready")
    e_ss = sem("edge_squares_summed")
    e_rb = sem("edge_var2_eps")
    e_r2 = sem("edge_rstd2")
    e_oe = sem("edge_output_ready")

    block = ctx.enter_context(nc.Block())

    x_steps = x[0:(G - 1) * STEP, :].rearrange("(g p j) d -> g p (j d)", p=P, j=ROWS)
    o_steps = out[0:(G - 1) * STEP, :].rearrange("(g p j) d -> g p (j d)", p=P, j=ROWS)
    x_rest = x[(G - 1) * STEP:N, :].rearrange("(p j) d -> p (j d)", j=REST_J)
    o_rest = out[(G - 1) * STEP:N, :].rearrange("(p j) d -> p (j d)", j=REST_J)
    attr_blocks = attr[0:(B - 1) * EB, :].rearrange("(b t p) r -> b p t r", t=2, p=P)
    ntype_rows = ntype.rearrange("(n a) -> n a", a=1)

    def cut_to(g_last, np_, nj):
        return (REST_P, REST_J) if g_last else (np_, nj)

    def own(eng, passed):
        eng.sem_inc(passed, 1)

    @block.sync
    def _(sp):
        with nc.allow_non_contiguous_dma(reason="bias columns, once"):
            sp.dma_start(wc[:], w_comb.rearrange("(c p) n -> p c n", p=P)).then_inc(s_w1, 16)
            sp.dma_start(bc[:], b_comb.rearrange("(a n) -> a n", a=1).to_broadcast([P, D])).then_inc(s_w1, 16)
            sp.dma_start(bff_row[:], b_ff.rearrange("(a n) -> a n", a=1).to_broadcast([P, D])).then_inc(s_w1, 16)
            sp.dma_start(xin[:, 0, :], x_steps[0]).then_inc(n_x[0], 16)
            sp.dma_start(xin[:, 1, :], x_steps[1]).then_inc(n_x[1], 16)
            sp.wait_ge(s_pad, 1)
            shifted = dst[1:E]
            for k, a in enumerate((src, dst, shifted)):
                n = a.shape[0]
                full = n // P
                sp.dma_start(rows_i[0:full, k, :], a[0:full * P].rearrange("(t p) -> t p", p=P)).then_inc(s_rows, 16)
                sp.dma_start(rows_i[full:full + 1, k, 0:n - full * P],
                             a[full * P:n].rearrange("(t p) -> t p", t=1)).then_inc(s_rows, 16)
            sp.dma_start(rows_f[0:FULL_T, 3, :], weight[0:FULL_T * P].rearrange("(t p) -> t p", p=P)).then_inc(s_rows, 16)
            sp.dma_start(rows_f[FULL_T:FULL_T + 1, 3, 0:REST_E],
                         weight[FULL_T * P:E].rearrange("(t p) -> t p", t=1)).then_inc(s_rows, 16)
            sp.dma_start(w_raw[:, 0:3 * DC, :], w_qkv.rearrange("(c p) n -> p c n", p=P)).then_inc(s_w, 16)
            sp.dma_start(w_raw[:, 3 * DC:, :], w_ff.rearrange("(c p) n -> p c n", p=P)).then_inc(s_w, 16)
            sp.dma_start(bff_col[:], b_ff.rearrange("(c p) -> p c", p=P)).then_inc(s_w, 16)
            sp.dma_start(bqkv[:], b_qkv.rearrange("(c p) -> p c", p=P)).then_inc(s_w, 16)
            sp.dma_start(wd[0:RBF, :], w_dist).then_inc(s_w, 16)
            sp.dma_start(wd[RBF:RBF + 1, :], b_dist.rearrange("(a n) -> a n", a=1)).then_inc(s_w, 16)
            sp.dma_start(tab[:], table).then_inc(s_w, 16)

        def store(h, par, last=False):
            sp.wait_ge(n_o, 2 * h + par + 1)
            if last:
                sp.dma_start(o_rest, on[0:REST_P, par, 0:REST_J * D]).then_inc(n_out[par], 16)
            else:
                sp.dma_start(o_steps[2 * h + par], on[:, par, :]).then_inc(n_out[par], 16)

        def load(h, par, last=False):
            sp.wait_ge(n_z, 2 * h + par - 1)
            if last:
                sp.dma_start(xin[0:REST_P, par, 0:REST_J * D], x_rest).then_inc(n_x[par], 16)
            else:
                sp.dma_start(xin[:, par, :], x_steps[2 * h + par]).then_inc(n_x[par], 16)

        with sp.Fori(1, G // 2 - 1) as h:
            for par in range(2):
                load(h, par)
                store(h - 1, par)
        for par in range(2):
            load(G // 2 - 1, par, last=par == 1)
            store(G // 2 - 2, par)
        for par in range(2):
            store(G // 2 - 1, par, last=par == 1)

        def load_attr(h, par):
            after(sp, e_atc, 3 * (2 * h + par - 1))
            sp.dma_start(at[:, par, :, :], attr_blocks[2 * h + par]).then_inc(e_at[par], 16)

        load_attr(0, 0)
        load_attr(0, 1)
        with sp.Fori(1, (B - 1) // 2) as h:
            for par in range(2):
                load_attr(h, par)
        sp.wait_ge(e_atc, 3 * (B - 2))
        e0 = (B - 1) * EB
        sp.dma_start(at[:, 0, 0, :], attr[e0:e0 + P, :]).then_inc(e_at[0], 16)
        sp.dma_start(at[0:REST_E, 0, 1, :], attr[e0 + P:E, :]).then_inc(e_at[0], 16)
        for par in range(2):
            sp.wait_ge(n_out[par], 16 * (G // 2))

    @block.gpsimd
    def _(pool):
        pool.memset(rows_i[:], -1).then_inc(s_const, 1)
        pool.memset(rows_f[:, 3, :], 0.0).then_inc(s_const, 1)
        pool.wait_ge(s_const, 2)
        pool.memset(ident[:], 0.0).then_inc(s_pad, 1)
        pool.memset(neg_half[:], -0.5).then_inc(s_const, 1)
        pool.memset(ones_mean[:], 1.0 / D).then_inc(s_const, 1)
        pool.wait_ge(s_pad, 1)
        pool.affine_select(out=ident[:], in_=ident[:], compare_op=ALU.not_equal, fill=1.0, base=0,
                           pattern=[[-1, P]], channel_multiplier=1).then_inc(s_id, 1)
        pool.wait_ge(s_const, 4)

        def z_add(h, par, np_=P, nj=ROWS):
            g = 2 * h + par
            pool.wait_ge(n_x[par], 16 * (h + 1))
            after(pool, n_tp, 2 * (g - 1))
            after(pool, n_st, g - 1)
            z = zin[0:np_, par, 0:nj * D].rearrange("p (j d) -> p j d", j=nj)
            xx = xin[0:np_, par, 0:nj * D].rearrange("p (j d) -> p j d", j=nj)
            bb = bff_row[0:np_, :].rearrange("p (a d) -> p a d", a=1).to_broadcast([np_, nj, D])
            pool.tensor_tensor(z, xx, bb, ALU.add).then_inc(n_z, 1)

        def rstd1(h, par, np_=P, nj=ROWS):
            g = 2 * h + par
            pool.wait_ge(n_mv, g + 1)
            after(pool, n_yy, g - 1)
            own(pool, s_pool_passed)
            pool.tensor_scalar(r1a[0:np_, par, 0:nj], mv[0:np_, par, 0:nj, 1], 1.0, EPS, ALU.mult, ALU.add).then_inc(n_ra, 1)
            pool.wait_ge(n_ra, g + 1)
            pool.tensor_tensor(r1[0:np_, par, 0:nj], r1a[0:np_, par, 0:nj], neg_half[0:np_, 0:nj], ALU.pow).then_inc(n_r1, 1)

        def rstd2(h, par, np_=P, nj=ROWS):
            g = 2 * h + par
            pool.wait_ge(n_ss, g + 1)
            after(pool, n_o, g - 1)
            own(pool, s_pool_passed)
            pool.tensor_scalar(r2a[0:np_, par, 0:nj], ss[0:np_, par, 0:nj], 1.0, EPS, ALU.mult, ALU.add).then_inc(n_rb, 1)
            pool.wait_ge(n_rb, g + 1)
            pool.tensor_tensor(r2[0:np_, par, 0:nj], r2a[0:np_, par, 0:nj], neg_half[0:np_, 0:nj], ALU.pow).then_inc(n_r2, 1)

        pool.iota(lane_i[:], [[0, 1]], base=0, channel_multiplier=1).then_inc(s_lane, 1)
        pool.wait_ge(s_w1, 16 * 3)
        z_add(0, 0)
        z_add(0, 1)
        rstd1(0, 0)

        def node(h, par, last=False):
            hn, pn = back(h, par, -1)
            if last:
                z_add(hn, pn, REST_P, REST_J)
            else:
                z_add(hn, pn)
            rstd1(h, par)
            hb, pb = back(h, par, 1)
            rstd2(hb, pb)

        node(0, 1)
        for par in range(2):
            node(1, par)
        with pool.Fori(2, G // 2 - 1) as h:
            for par in range(2):
                node(h, par)
        node(G // 2 - 1, 0, last=True)
        rstd1(G // 2 - 1, 1, REST_P, REST_J)
        rstd2(G // 2 - 1, 0)
        rstd2(G // 2 - 1, 1, REST_P, REST_J)

        def indices(h, par):
            b = 2 * h + par
            after(pool, e_g[par], 96 * h)
            after(pool, e_bcp, b - 1)
            own(pool, s_pool_passed)
            pool.tensor_copy(idx_b[:, par, :], idx[:, b, :]).then_inc(e_idx, 1)
            pool.tensor_copy(fcol_b[:, par, :], fcol[:, b, :]).then_inc(e_fc, 1)

        def gathers(h, par):
            b = 2 * h + par
            pool.wait_ge(e_idx, b + 1)
            after(pool, e_xsp, b - 1)
            after(pool, e_xdp, b - 1)
            after(pool, e_ty, b - 1)
            own(pool, s_pool_passed)
            for t in range(2):
                pool.indirect_dma_start(xs[:, par, t, :], None, x, bass.IndirectOffsetOnAxis(idx_b[:, par, t:t + 1], 0)).then_inc(e_g[par], 16)
                pool.indirect_dma_start(xd[:, par, t, :], None, x, bass.IndirectOffsetOnAxis(idx_b[:, par, 2 + t:3 + t], 0)).then_inc(e_g[par], 16)
                pool.indirect_dma_start(ty[:, par, t:t + 1], None, ntype_rows,
                                        bass.IndirectOffsetOnAxis(idx_b[:, par, t:t + 1], 0)).then_inc(e_g[par], 16)

        def float_types(h, par):
            b = 2 * h + par
            pool.wait_ge(e_g[par], 96 * (h + 1))
            after(pool, e_bcp, b - 1)
            own(pool, s_pool_passed)
            pool.tensor_copy(ty_f[:, par, :], ty[:, par, :]).then_inc(e_ty, 1)

        def scale_attr(h, par, partial=False):
            b = 2 * h + par
            after(pool, e_atp, b)
            pool.wait_ge(e_at[par], 16 * (h + (2 if partial else 1)))
            pool.wait_ge(e_fc, b + 1)
            own(pool, s_pool_passed)
            for t in range(2):
                pool.tensor_scalar(atc[:, t, 0:RBF], at[:, par, t, :], fcol_b[:, par, t:t + 1], None, ALU.mult).then_inc(e_atc, 1)
            pool.tensor_copy(atc[:, :, RBF], fcol_b[:, par, 0:2]).then_inc(e_atc, 1)

        def drop(h, par):
            b = 2 * h + par
            pool.wait_ge(e_m, 2 * (b + 1))
            pool.wait_ge(e_m0, b + 1)
            pool.wait_ge(e_neg, b + 1)
            nb = neg[:, par, :].rearrange("p (a n) -> p a n", a=1).to_broadcast([P, 2, EB])
            pool.tensor_tensor(ua[:], mx[:, par, :, 0:EB], nb, ALU.add).then_inc(e_ua, 1)
            pool.wait_ge(e_ua, b + 1)
            after(pool, e_resc, b)
            pool.tensor_tensor(ub[:], ua[:], mx[:, par, :, 1:EB + 1], ALU.subtract).then_inc(e_u, 1)

        def weigh(h, par):
            b = 2 * h + par
            pool.wait_ge(e_ex, b + 1)
            pool.wait_ge(e_v, 2 * (b + 1))
            after(pool, e_num, 2 * b)
            pool.tensor_tensor(ev[:], ex[:], vT[:], ALU.mult).then_inc(e_ev, 1)

        def edge_rstd1(h, par):
            b = 2 * h + par
            pool.wait_ge(e_mv, 2 * (b + 1))
            after(pool, e_y, 2 * b)
            own(pool, s_pool_passed)
            pool.tensor_scalar(er1a[:], emv[:, :, 1], 1.0, EPS, ALU.mult, ALU.add).then_inc(e_ra, 1)
            pool.wait_ge(e_ra, b + 1)
            pool.tensor_tensor(er1[:], er1a[:], neg_half[:, 0:2], ALU.pow).then_inc(e_r1, 1)

        def edge_rstd2(h, par):
            b = 2 * h + par
            pool.wait_ge(e_ss, 2 * (b + 1))
            after(pool, e_oe, 2 * b)
            own(pool, s_pool_passed)
            pool.tensor_scalar(er2a[:], ess[:], 1.0, EPS, ALU.mult, ALU.add).then_inc(e_rb, 1)
            pool.wait_ge(e_rb, b + 1)
            pool.tensor_tensor(er2[:], er2a[:], neg_half[:, 0:2], ALU.pow).then_inc(e_r2, 1)

        def scatter_indices(h, par):
            b = 2 * h + par
            own(pool, s_pool_passed)
            pool.tensor_copy(idx_b[:, 2, 2 * par:2 * par + 2], idx[:, b, 4:6]).then_inc(e_sci, 1)

        def scatter(h, par):
            b = 2 * h + par
            pool.wait_ge(e_sci, b + 1)
            pool.wait_ge(e_oe, 2 * (b + 1))
            own(pool, s_pool_passed)
            for t in range(2):
                pool.indirect_dma_start(out, bass.IndirectOffsetOnAxis(idx_b[:, 2, 2 * par + t:2 * par + t + 1], 0), oe[:, par, t, :], None,
                                        bounds_check=N - 1, oob_is_err=False).then_inc(e_sc[par], 16)

        def edge(h, par, now=True, ahead=True, one=True, two=True):
            hn, pn = back(h, par, -1)
            h1, p1 = back(h, par, 1)
            h2, p2 = back(h, par, 2)
            if now:
                float_types(h, par)
                scale_attr(h, par, partial=not ahead)
            if ahead:
                indices(hn, pn)
            if two:
                edge_rstd2(h2, p2)
                after(pool, e_sc[p2], 16 * 2 * h2)
                scatter_indices(h2, p2)
            if ahead:
                gathers(hn, pn)
            if two:
                scatter(h2, p2)
            if now:
                drop(h, par)
            if one:
                edge_rstd1(h1, p1)
            if now:
                weigh(h, par)

        pool.wait_ge(s_idx, 1)
        indices(0, 0)
        gathers(0, 0)
        for par in range(2):
            pool.wait_ge(n_out[par], 16 * (G // 2))
        edge(0, 0, one=False, two=False)
        edge(0, 1, two=False)
        for par in range(2):
            edge(1, par)
        with pool.Fori(2, (B - 1) // 2) as h:
            for par in range(2):
                edge(h, par)
        L = (B - 1) // 2
        edge(L, 0, ahead=False)
        edge(L, 1, now=False, ahead=False)
        edge(L + 1, 0, now=False, ahead=False, one=False)
        pool.wait_ge(e_sc[0], 16 * 2 * (L + 1))
        pool.wait_ge(e_sc[1], 16 * 2 * L)

    @block.tensor
    def _(pe):
        mm = pe.matmul
        pe.wait_ge(s_id, 1)
        pe.wait_ge(s_w, 16 * 7)
        for k in range(DC):
            for r in range(4 * DC):
                pe.transpose(ps[:, 4 + 2 * k + r // 4, (r % 4) * P:(r % 4 + 1) * P],
                             w_raw[:, r, k * P:(k + 1) * P], ident[:]).then_inc(s_wtp, 1)
        pe.wait_ge(s_wchain, 7)
        for k in range(DC):
            last = mm(ps[:, 0, 0:D], ones_mean[:], wc[:, k, :], start=k == 0, stop=k == DC - 1)
        last.then_inc(s_cm, 1)
        pe.wait_ge(s_ef, 1)
        for k in range(4):
            last = pe.transpose(ps[:, 1, k * T:(k + 1) * T], rows_f[:, k, :], ident[0:T, 0:T])
        last.then_inc(s_ep, 1)

        def z_transposes(h, par, np_=P, nj=ROWS):
            g = 2 * h + par
            pe.wait_ge(n_z, g + 1)
            for c in range(DC):
                after(pe, n_tc, 2 * (g - 1))
                for j in range(nj):
                    last = pe.transpose(ps[:, 2 * par + c, j * P:j * P + np_],
                                        zin[0:np_, par, j * D + c * P:j * D + (c + 1) * P], ident[0:np_, 0:np_])
                last.then_inc(n_tp, 1)

        def z_product(h, par, np_=P, nj=ROWS):
            g = 2 * h + par
            pe.wait_ge(n_tc, 2 * (g + 1))
            after(pe, n_yy, g - 1)
            for j in range(nj):
                for k in range(DC):
                    last = mm(ps[0:np_, 4 + 2 * par + j // 2, (j % 2) * D:(j % 2 + 1) * D],
                              zT[:, par, k, j * P:j * P + np_], w_mix[:, k, :], start=k == 0, stop=k == DC - 1)
                if j % 2 == 1 or j == nj - 1:
                    last.then_inc(n_y, 1)

        pe.wait_ge(s_ec, 1)
        pe.wait_ge(s_wtc, 4)
        pe.wait_ge(s_wready, 2)
        z_transposes(0, 0)
        z_transposes(0, 1)
        z_product(0, 0)

        def node(h, par, last=False):
            hn, pn = back(h, par, -1)
            if last:
                z_transposes(hn, pn, REST_P, REST_J)
            else:
                z_transposes(hn, pn)
            z_product(h, par)

        node(0, 1)
        for par in range(2):
            node(1, par)
        with pe.Fori(2, G // 2 - 1) as h:
            for par in range(2):
                node(h, par)
        node(G // 2 - 1, 0, last=True)
        z_product(G // 2 - 1, 1, REST_P, REST_J)

        def project(out_bank, weights, moving, done):
            for c in range(2):
                for k in range(DC):
                    last = mm(bank(out_bank)[:, c, :], wT[:, k, weights + c * P:weights + (c + 1) * P], moving[:, k, :],
                              start=k == 0, stop=k == DC - 1)
            last.then_inc(done, 1)

        def edge(h, par, now=True, one=True):
            b = 2 * h + par
            h1, p1 = back(h, par, 1)
            b1 = 2 * h1 + p1
            if now:
                pe.wait_ge(e_fc, b + 1)
                pe.wait_ge(e_ty, b + 1)
                after(pe, e_st, b - 1)
                for t in range(2):
                    pe.transpose(ps[:, 0, t * P:(t + 1) * P], fcol_b[:, par, 2 + t:3 + t].to_broadcast([P, P]), ident[:])
                for t in range(2):
                    last = pe.transpose(ps[:, 0, EB + t * P:EB + (t + 1) * P], ty_f[:, par, t:t + 1].to_broadcast([P, P]), ident[:])
                last.then_inc(e_bcp, 1)
                pe.wait_ge(e_g[par], 96 * (h + 1))
                after(pe, e_z, 2 * (b - 1))
                for c in range(DC):
                    for t in range(2):
                        last = pe.transpose(bank(1)[:, c, t * P:(t + 1) * P], xs[:, par, t, c * P:(c + 1) * P], ident[:])
                last.then_inc(e_xsp, 1)
                after(pe, e_emb, b)
                for c in range(DC):
                    for t in range(2):
                        last = pe.transpose(bank(2)[:, c, t * P:(t + 1) * P], xd[:, par, t, c * P:(c + 1) * P], ident[:])
                last.then_inc(e_xdp, 1)
            if one:
                pe.wait_ge(e_den, 2 * (b1 + 1))
                after(pe, e_rd, b1)
                for t in range(2):
                    for c in range(DC):
                        o = (2 * t + c) * HPC
                        last = mm(ps[:, 7, o:o + HPC], den[:, p1, c, t * P:(t + 1) * P], ident[:, 0:P:HD], start=True, stop=True)
                last.then_inc(e_denp, 1)
            if now:
                pe.wait_ge(e_xdc, b + 1)
                after(pe, e_t2, b - 1)
                project(3, 0, xdT[:, par], e_qp)
                pe.wait_ge(e_xsc, b + 1)
                after(pe, e_msg, b)
                project(4, D, xsT, e_kp)
            if one:
                pe.wait_ge(e_rdx, b1 + 1)
                pe.wait_ge(e_d, b1 + 1)
                for c in range(DC):
                    for t in range(2):
                        last = pe.transpose(bank(6)[:, c, t * P:(t + 1) * P],
                                            rdx[:, t, c, :], ident[:])
                last.then_inc(e_rdp, 1)
            if now:
                after(pe, e_y, 2 * (b - 1))
                project(5, 2 * D, xsT, e_vp)
                pe.wait_ge(e_atc, 3 * (b + 1))
                pe.wait_ge(e_dbc, 2 * (b + 1))
                pe.wait_ge(e_hot, b + 1)
                for t in range(2):
                    last = pe.transpose(ps[0:RBF + 1, 0, t * P:(t + 1) * P], atc[:, t, :], ident[:])
                last.then_inc(e_atp, 1)
            if one:
                pe.wait_ge(e_o, b1 + 1)
                if now:
                    pe.wait_ge(e_xsc, b + 1)
                project(1, 3 * D, oT, e_ffp)
            if now:
                pe.wait_ge(e_hot, b + 1)
                pe.wait_ge(e_xdc, b + 1)
                for c in range(2):
                    for s in range(3):
                        last = mm(bank(2)[:, c, :], tab3[:, s, c * P:(c + 1) * P], hot[0:SPECIES, :], start=s == 0, stop=s == 2)
                last.then_inc(e_embp, 1)
                pe.wait_ge(e_prod, 2 * (b + 1))
                if one:
                    pe.wait_ge(e_o, b1 + 1)
                for c in range(2):
                    last = mm(bank(6)[:, c, :], head_sum[:], prod[:, c, :], start=True, stop=True)
                last.then_inc(e_attp, 1)
            if one:
                pe.wait_ge(e_agg, 2 * (b1 + 1))
                if now:
                    pe.wait_ge(e_q, 2 * (b + 1))
                for t in range(2):
                    for k in range(DC):
                        last = mm(bank(3)[:, t, :], agg[:, p1, k, t * P:(t + 1) * P], wc[:, 2 + k, :], start=k == 0, stop=k == DC - 1)
                last.then_inc(e_aggp, 1)
            if now:
                pe.wait_ge(e_atT, b + 1)
                for c in range(2):
                    last = mm(bank(4)[:, c, :], wd[:, c * P:(c + 1) * P], atT[:], start=True, stop=True)
                last.then_inc(e_wdp, 1)
            if one:
                pe.wait_ge(e_z, 2 * (b1 + 1))
                for t in range(2):
                    for c in range(DC):
                        last = pe.transpose(bank(0)[:, t, c * P:(c + 1) * P], zeT[:, c, t * P:(t + 1) * P], ident[:])
                last.then_inc(e_zp, 1)
                if now:
                    pe.wait_ge(e_v, 2 * (b + 1))
                for t in range(2):
                    for k in range(DC):
                        last = mm(bank(5)[:, t, :], zeT[:, k, t * P:(t + 1) * P], w_mix[:, k, :], start=k == 0, stop=k == DC - 1)
                last.then_inc(e_mixp, 1)

        pe.wait_ge(n_yy, G)
        edge(0, 0, one=False)
        edge(0, 1)
        for par in range(2):
            edge(1, par)
        with pe.Fori(2, (B - 1) // 2) as h:
            for par in range(2):
                edge(h, par)
        L = (B - 1) // 2
        edge(L, 0)
        edge(L, 1, now=False)

    @block.scalar
    def _(act):
        for k in range(DC):
            for r in range(2):
                act.wait_ge(s_wtp, 8 * k + 4 * r + 4)
                act.activation(wT[:, k, r * 512:(r + 1) * 512], ps[:, 4 + 2 * k + r, :], ACT.Copy).then_inc(s_wtc, 1)
        act.wait_ge(s_echain, 7)
        act.activation(ct[:, 3, :], ct[:, 2, :], ACT.Sin, bias=half_pi[:], scale=-float(np.pi) / CUTOFF).then_inc(s_sin, 1)

        def zT_copy(h, par):
            g = 2 * h + par
            for c in range(DC):
                act.wait_ge(n_tp, 2 * g + c + 1)
                after(act, n_y, 2 * (g - 1))
                act.activation(zT[:, par, c, :], ps[:, 2 * par + c, :], ACT.Copy).then_inc(n_tc, 1)

        def squares(h, par, np_=P, nj=ROWS):
            g = 2 * h + par
            act.wait_ge(n_yy, g + 1)
            after(act, n_rb, g - 1)
            after(act, n_ss, g)
            for j in range(nj):
                last = act.activation(junk[0:np_, j, :], yn[0:np_, par, j * D:(j + 1) * D], ACT.Square,
                                      scale=float(D ** -0.5), accum_out=ss[0:np_, par, j:j + 1])
            last.then_inc(n_ss, 1)

        zT_copy(0, 0)
        zT_copy(0, 1)
        squares(0, 0)

        def node(h, par):
            zT_copy(*back(h, par, -1))
            squares(h, par)

        node(0, 1)
        for par in range(2):
            node(1, par)
        with act.Fori(2, G // 2 - 1) as h:
            for par in range(2):
                node(h, par)
        node(G // 2 - 1, 0)
        squares(G // 2 - 1, 1, REST_P, REST_J)

        def edge(h, par, now=True, one=True, two=True):
            b = 2 * h + par
            h1, p1 = back(h, par, 1)
            b1 = 2 * h1 + p1
            h2, p2 = back(h, par, 2)
            b2 = 2 * h2 + p2
            if now:
                after(act, e_same, b - 1)
                after(act, e_dbc, 2 * b)
                act.activation(dbc[:, par, 0:1], dbc[:, 1 - par, EB:EB + 1], ACT.Copy).then_inc(e_dbc, 1)
                act.wait_ge(e_bcp, b + 1)
                act.activation(dbc[:, par, 1:EB + 1], ps[:, 0, 0:EB], ACT.Copy).then_inc(e_dbc, 1)
                act.wait_ge(e_xsp, b + 1)
                after(act, e_vp, b)
                act.activation(xsT[:].rearrange("p c n -> p (c n)"), ps[:, 1, :], ACT.Copy).then_inc(e_xsc, 1)
                act.wait_ge(e_xdp, b + 1)
                after(act, e_z, 2 * (b - 1))
                act.activation(xdT[:, par].rearrange("p c n -> p (c n)"), ps[:, 2, :], ACT.Copy).then_inc(e_xdc, 1)
            if one:
                act.wait_ge(e_rd, b1 + 1)
                after(act, e_rdp, b1)
                act.activation(rdx[:].rearrange("p t c (h a) -> p (t c h) a", a=HD),
                               rd[:].rearrange("p t c (h a) -> p (t c h) a", a=1).to_broadcast([P, 4 * HPC, HD]), ACT.Copy).then_inc(e_rdx, 1)
            if now:
                act.wait_ge(e_qp, b + 1)
                after(act, e_prod, 2 * b)
                for c in range(2):
                    act.activation(qT[:, c, :], bank(3)[:, c, :], ACT.Identity, bias=bqkv[:, c:c + 1]).then_inc(e_q, 1)
                act.wait_ge(e_vp, b + 1)
                after(act, e_ev, b)
                for c in range(2):
                    act.activation(vT[:, c, :], bank(5)[:, c, :], ACT.Identity, bias=bqkv[:, 4 + c:5 + c]).then_inc(e_v, 1)
            if two:
                act.wait_ge(e_y, 2 * (b2 + 1))
                after(act, e_rb, b2)
                after(act, e_ss, 2 * b2)
                act.wait_ge(n_ss, G)
                for t in range(2):
                    act.activation(junk[:, t, :], ye[:, p2, t, :], ACT.Square, scale=float(D ** -0.5), accum_out=ess[:, t:t + 1]).then_inc(e_ss, 1)
            if now:
                act.wait_ge(e_atp, b + 1)
                after(act, e_wdp, b)
                act.activation(atT[:], ps[0:RBF + 1, 0, 0:EB], ACT.Copy).then_inc(e_atT, 1)
                act.wait_ge(e_embp, b + 1)
                after(act, e_msg, b)
                act.activation(emb[:].rearrange("p c n -> p (c n)"), ps[:, 2, :], ACT.Copy).then_inc(e_emb, 1)
            if two:
                act.wait_ge(e_r2, b2 + 1)
                after(act, e_sc[p2], 32 * h2)
                for t in range(2):
                    act.activation(oe[:, p2, t, :], ye[:, p2, t, :], ACT.Copy, scale=er2[:, t:t + 1]).then_inc(e_oe, 1)
            if now:
                act.wait_ge(e_u, b + 1)
                after(act, e_num, 2 * b)
                act.activation(resc[:], ub[:], ACT.Exp, scale=SCALE).then_inc(e_resc, 1)
                act.wait_ge(e_d, b + 1)
                after(act, e_ev, b)
                act.activation(ex[:], dlt[:], ACT.Exp, scale=SCALE).then_inc(e_ex, 1)

        edge(0, 0, one=False, two=False)
        edge(0, 1, two=False)
        for par in range(2):
            edge(1, par)
        with act.Fori(2, (B - 1) // 2) as h:
            for par in range(2):
                edge(h, par)
        L = (B - 1) // 2
        edge(L, 0)
        edge(L, 1, now=False)
        edge(L + 1, 0, now=False, one=False)

    @block.vector
    def _(dve):
        dve.memset(head_sum[:], 0.0).then_inc(s_hs, 1)
        dve.memset(half_pi[:], float(np.pi) / 2).then_inc(s_hs, 1)
        for a in (mx, den, num, agg):
            dve.memset(a[:, 1], 0.0).then_inc(s_hs, 1)
        dve.memset(dbc[:, 1, EB:EB + 1], -5.0).then_inc(s_hs, 1)
        dve.wait_ge(s_hs, 7)
        for q in range(HPC):
            dve.memset(head_sum[q * HD:(q + 1) * HD, q * HD:(q + 1) * HD], 1.0).then_inc(s_hs, 1)

        dve.wait_ge(s_w1, 16 * 3)
        dve.wait_ge(s_id, 1)
        for c in range(DC):
            dve.tensor_tensor(wc[:, c, c * P:(c + 1) * P], wc[:, c, c * P:(c + 1) * P], ident[:], ALU.add).then_inc(s_wchain, 1)
        dve.wait_ge(s_wchain, 2)
        dve.tensor_reduce(wc_mean[:], wc[:], AX.X, ALU.add).then_inc(s_wsum, 1)
        dve.tensor_reduce(bc_mean[:], bc[:], AX.X, ALU.add).then_inc(s_wsum, 1)
        dve.wait_ge(s_wsum, 2)
        dve.tensor_scalar(wc_mean[:], wc_mean[:], 1.0 / D, None, ALU.mult).then_inc(s_wsum, 1)
        dve.tensor_scalar(bc_mean[:], bc_mean[:], 1.0 / D, None, ALU.mult).then_inc(s_wsum, 1)
        dve.wait_ge(s_wsum, 4)
        for c in range(2 * DC):
            dve.tensor_scalar(wc[:, c, :], wc[:, c, :], wc_mean[:, c:c + 1], None, ALU.subtract).then_inc(s_wchain, 1)
        dve.tensor_scalar(bc[:], bc[:], bc_mean[:], None, ALU.subtract).then_inc(s_wchain, 1)
        dve.wait_ge(s_cm, 1)
        for c in range(DC):
            dve.tensor_tensor(w_mix[:, c, :], wc[:, c, :], ps[:, 0, 0:D], ALU.subtract).then_inc(s_wready, 1)

        dve.wait_ge(s_rows, 16 * 8)
        dve.tensor_copy(rows_f[:, 0:3, :], rows_i[:]).then_inc(s_ef, 1)
        dve.wait_ge(s_ep, 1)
        dve.tensor_copy(cols[:].rearrange("p k t -> p (k t)"), ps[:, 1, 0:4 * T]).then_inc(s_ec, 1)
        dve.wait_ge(s_ec, 1)
        dve.scalar_tensor_tensor(out=ct[:, 0, :], in0=cols[:, 3, :], scalar=-1.0, in1=cols[:, 3, :], op0=ALU.mult, op1=ALU.max).then_inc(s_echain, 1)
        dve.wait_ge(s_echain, 1)
        dve.tensor_scalar(ct_i[:], ct[:, 0, :], 0.5 / CUTOFF, None, ALU.mult).then_inc(s_echain, 1)
        dve.wait_ge(s_echain, 2)
        dve.tensor_copy(ct[:, 1, :], ct_i[:]).then_inc(s_echain, 1)
        dve.wait_ge(s_echain, 3)
        dve.scalar_tensor_tensor(out=ct[:, 2, :], in0=ct[:, 1, :], scalar=-2.0 * CUTOFF, in1=ct[:, 0, :], op0=ALU.mult, op1=ALU.add).then_inc(s_echain, 1)
        dve.wait_ge(s_echain, 4)
        dve.scalar_tensor_tensor(out=ct[:, 0, :], in0=ct[:, 2, :], scalar=-1.0, in1=ct[:, 2, :], op0=ALU.mult, op1=ALU.max).then_inc(s_echain, 1)
        dve.wait_ge(s_echain, 5)
        dve.tensor_scalar(ct[:, 1, :], ct[:, 0, :], -1.0, 2.0 * CUTOFF, ALU.mult, ALU.add).then_inc(s_echain, 1)
        dve.wait_ge(s_echain, 6)
        dve.tensor_tensor(ct[:, 2, :], ct[:, 0, :], ct[:, 1, :], ALU.min).then_inc(s_echain, 1)
        dve.wait_ge(s_sin, 1)
        dve.tensor_scalar(ct[:, 0, :], ct[:, 3, :], 0.5, 0.5, ALU.mult, ALU.add).then_inc(s_echain, 1)
        dve.tensor_tensor(ct[:, 1, :], cols[:, 1, :], cols[:, 2, :], ALU.is_equal).then_inc(s_echain, 1)
        dve.wait_ge(s_echain, 9)

        def pairs(a):
            return a.rearrange("p (b t) -> p b t", t=2)

        dve.scalar_tensor_tensor(out=fcol[:, :, 0:2], in0=pairs(cols[:, 3, :]), scalar=CUTOFF, in1=pairs(ct[:, 0, :]), op0=ALU.is_lt, op1=ALU.mult).then_inc(s_echain, 1)
        dve.scalar_tensor_tensor(out=idx[:, :, 4:6], in0=pairs(ct[:, 1, :]), scalar=SKIP, in1=pairs(cols[:, 1, :]), op0=ALU.mult, op1=ALU.add).then_inc(s_echain, 1)
        dve.tensor_copy(fcol[:, :, 2:4], pairs(cols[:, 1, :])).then_inc(s_echain, 1)
        for k in range(2):
            dve.tensor_scalar(idx[:, :, 2 * k:2 * k + 2], pairs(cols[:, k, :]), 0.0, None, ALU.max).then_inc(s_echain, 1)
        dve.wait_ge(s_echain, 14)
        dve.wait_ge(s_w, 16 * 7)
        dve.tensor_copy(tab3[:, 0, :], tab[:]).then_inc(s_tab, 1)
        dve.wait_ge(s_tab, 1)
        dve.tensor_tensor(tab_res[:], tab[:], tab3[:, 0, :], ALU.subtract).then_inc(s_tab, 1)
        dve.wait_ge(s_tab, 2)
        dve.tensor_copy(tab3[:, 1, :], tab_res[:]).then_inc(s_tab, 1)
        dve.wait_ge(s_tab, 3)
        dve.tensor_tensor(tab[:], tab_res[:], tab3[:, 1, :], ALU.subtract).then_inc(s_tab, 1)
        dve.wait_ge(s_tab, 4)
        dve.tensor_copy(tab3[:, 2, :], tab[:]).then_inc(s_tab, 1)
        dve.wait_ge(s_tab, 5)
        dve.wait_ge(s_lane, 1)
        dve.tensor_copy(lane[:], lane_i[:]).then_inc(s_idx, 1)

        def stats(h, par, np_=P, nj=ROWS):
            g = 2 * h + par
            dve.wait_ge(n_z, g + 1)
            after(dve, n_mv, g - 1)
            for j in range(nj):
                last = dve.bn_stats(stat[0:np_, par, j, :], zin[0:np_, par, j * D:(j + 1) * D])
            last.then_inc(n_st, 1)
            dve.wait_ge(n_st, g + 1)
            after(dve, n_ra, g - 1)
            own(dve, s_dve_passed)
            for j in range(nj):
                last = dve.bn_aggr(mv[0:np_, par, j, :], stat[0:np_, par, j, :])
            last.then_inc(n_mv, 1)

        def y(h, par, np_=P, nj=ROWS):
            g = 2 * h + par
            dve.wait_ge(n_r1, g + 1)
            after(dve, n_ss, g - 1)
            after(dve, n_o, g - 1)
            for j in range(nj):
                if j % 2 == 0:
                    dve.wait_ge(n_y, 2 * g + j // 2 + 1)
                last = dve.scalar_tensor_tensor(out=yn[0:np_, par, j * D:(j + 1) * D],
                                                in0=ps[0:np_, 4 + 2 * par + j // 2, (j % 2) * D:(j % 2 + 1) * D],
                                                scalar=r1[0:np_, par, j:j + 1], in1=bc[0:np_, :], op0=ALU.mult, op1=ALU.add)
            last.then_inc(n_yy, 1)

        def final(h, par, np_=P, nj=ROWS):
            g = 2 * h + par
            dve.wait_ge(n_r2, g + 1)
            dve.wait_ge(n_yy, g + 1)
            after(dve, n_out[par], 16 * h)
            for j in range(nj):
                last = dve.tensor_scalar(on[0:np_, par, j * D:(j + 1) * D], yn[0:np_, par, j * D:(j + 1) * D],
                                         r2[0:np_, par, j:j + 1], None, ALU.mult)
            last.then_inc(n_o, 1)

        stats(0, 0)
        stats(0, 1)
        y(0, 0)

        def node(h, par, last=False):
            hn, pn = back(h, par, -1)
            if last:
                stats(hn, pn, REST_P, REST_J)
            else:
                stats(hn, pn)
            y(h, par)
            final(*back(h, par, 1))

        node(0, 1)
        for par in range(2):
            node(1, par)
        with dve.Fori(2, G // 2 - 1) as h:
            for par in range(2):
                node(h, par)
        node(G // 2 - 1, 0, last=True)
        y(G // 2 - 1, 1, REST_P, REST_J)
        final(G // 2 - 1, 0)
        final(G // 2 - 1, 1, REST_P, REST_J)

        def edge(h, par, now=True, one=True):
            b = 2 * h + par
            h1, p1 = back(h, par, 1)
            b1 = 2 * h1 + p1
            if now:
                dve.wait_ge(e_bcp, b + 1)
                dve.wait_ge(e_dbc, 2 * (b + 1))
                after(dve, e_embp, b)
                dve.tensor_scalar(hot[0:SPECIES, :], ps[0:SPECIES, 0, EB:2 * EB], lane[0:SPECIES, 0:1], None, ALU.is_equal).then_inc(e_hot, 1)
                dve.tensor_tensor(same[:, par, :], dbc[:, par, 1:EB + 1], dbc[:, par, 0:EB], ALU.is_equal).then_inc(e_same, 1)
                dve.wait_ge(e_same, b + 1)
                after(dve, e_ua, b - 1)
                dve.tensor_scalar(neg[:, par, :], same[:, par, :], -1.0, FAR, ALU.add, ALU.mult).then_inc(e_neg, 1)
            if one:
                dve.wait_ge(e_denp, b1 + 1)
                after(dve, e_rdx, b1)
                dve.reciprocal(rd[:].rearrange("p t c h -> p (t c h)"), ps[:, 7, 0:4 * HPC]).then_inc(e_rd, 1)
            if now:
                dve.wait_ge(e_kp, b + 1)
                after(dve, e_attp, b)
                for c in range(2):
                    dve.wait_ge(e_q, 2 * b + c + 1)
                    dve.scalar_tensor_tensor(out=prod[:, c, :], in0=bank(4)[:, c, :], scalar=bqkv[:, 2 + c:3 + c], in1=qT[:, c, :],
                                             op0=ALU.add, op1=ALU.mult).then_inc(e_prod, 1)
            if one:
                dve.wait_ge(e_rdp, b1 + 1)
                dve.wait_ge(e_num, 2 * (b1 + 1))
                after(dve, e_ffp, b1)
                dve.tensor_tensor(oT[:], bank(6), num[:, p1], ALU.mult).then_inc(e_o, 1)
                dve.wait_ge(e_ffp, b1 + 1)
                after(dve, e_mixp, b1)
                for c in range(2):
                    dve.scalar_tensor_tensor(out=zeT[:, c, :], in0=bank(1)[:, c, :], scalar=bff_col[:, c:c + 1], in1=xdT[:, p1, c, :],
                                             op0=ALU.add, op1=ALU.add).then_inc(e_z, 1)
            if now:
                after(dve, e_m, 2 * b)
                after(dve, e_u, b - 1)
                dve.tensor_copy(mx[:, par, :, 0:1], mx[:, 1 - par, :, EB:EB + 1]).then_inc(e_m0, 1)
                dve.wait_ge(e_m0, b + 1)
                dve.wait_ge(e_neg, b + 1)
                dve.wait_ge(e_attp, b + 1)
                for c in range(2):
                    dve.tensor_tensor_scan(out=mx[:, par, c, 1:EB + 1], data0=neg[:, par, :], data1=bank(6)[:, c, :],
                                           initial=mx[:, par, c, 0:1], op0=ALU.add, op1=ALU.max).then_inc(e_m, 1)
                dve.wait_ge(e_m, 2 * (b + 1))
                after(dve, e_ex, b)
                dve.tensor_tensor(dlt[:], bank(6), mx[:, par, :, 1:EB + 1], ALU.subtract).then_inc(e_d, 1)
                dve.wait_ge(e_wdp, b + 1)
                dve.wait_ge(e_emb, b + 1)
                dve.tensor_tensor(msg[:], bank(4), emb[:], ALU.mult).then_inc(e_msg, 1)
            if one:
                dve.wait_ge(e_zp, b1 + 1)
                for t in range(2):
                    last = dve.bn_stats(est[:, t, :], bank(0)[:, t, :])
                last.then_inc(e_st, 1)
                dve.wait_ge(e_st, b1 + 1)
                after(dve, e_ra, b1)
                own(dve, s_dve_passed)
                for t in range(2):
                    dve.bn_aggr(emv[:, t, :], est[:, t, :]).then_inc(e_mv, 1)
                dve.wait_ge(e_aggp, b1 + 1)
                after(dve, e_y, 2 * b1)
                dve.tensor_tensor(t2[:], bank(3), bc[:].rearrange("p (a d) -> p a d", a=1).to_broadcast([P, 2, D]), ALU.add).then_inc(e_t2, 1)
            if now:
                dve.wait_ge(e_resc, b + 1)
                dve.wait_ge(e_ex, b + 1)
                after(dve, e_denp, b - 1)
                for c in range(2):
                    after(dve, e_den, 2 * b)
                    dve.tensor_tensor_scan(out=den[:, par, c, :], data0=resc[:, c, :], data1=ex[:, c, :],
                                           initial=den[:, 1 - par, c, EB - 1:EB], op0=ALU.mult, op1=ALU.add).then_inc(e_den, 1)
                dve.wait_ge(e_ev, b + 1)
                after(dve, e_num, 2 * b)
                for c in range(2):
                    dve.tensor_tensor_scan(out=num[:, par, c, :], data0=resc[:, c, :], data1=ev[:, c, :],
                                           initial=num[:, 1 - par, c, EB - 1:EB], op0=ALU.mult, op1=ALU.add).then_inc(e_num, 1)
                dve.wait_ge(e_msg, b + 1)
                after(dve, e_aggp, b - 1)
                after(dve, e_agg, 2 * b)
                for c in range(2):
                    dve.tensor_tensor_scan(out=agg[:, par, c, :], data0=same[:, par, :], data1=msg[:, c, :],
                                           initial=agg[:, 1 - par, c, EB - 1:EB], op0=ALU.mult, op1=ALU.add).then_inc(e_agg, 1)
            if one:
                dve.wait_ge(e_mixp, b1 + 1)
                dve.wait_ge(e_r1, b1 + 1)
                dve.wait_ge(e_t2, b1 + 1)
                after(dve, e_oe, 2 * (b1 - 1))
                for t in range(2):
                    dve.scalar_tensor_tensor(out=ye[:, p1, t, :], in0=bank(5)[:, t, :], scalar=er1[:, t:t + 1], in1=t2[:, t, :],
                                             op0=ALU.mult, op1=ALU.add).then_inc(e_y, 1)

        edge(0, 0, one=False)
        edge(0, 1)
        for par in range(2):
            edge(1, par)
        with dve.Fori(2, (B - 1) // 2) as h:
            for par in range(2):
                edge(h, par)
        L = (B - 1) // 2
        edge(L, 0)
        edge(L, 1, now=False)

    ctx.close()


_INS = ["x", "src", "dst", "edge_attr_64", "edge_weight", "node_type_100", "L0_gnn_W_qkv", "L0_gnn_b_qkv", "L0_gnn_W_ff",
        "L0_gnn_b_ff", "L1_gnn_embed_table", "L1_gnn_W_dist", "L1_gnn_b_dist", "L1_gnn_W_comb", "L1_gnn_b_comb"]


def kernel(**inputs):
    import numpy as _np
    import concourse.bacc as _bacc
    from concourse import mybir as _mybir
    from concourse.bass_utils import run_bass_kernel_spmd as _run

    nc = _bacc.Bacc("TRN2", target_bir_lowering=False, num_devices=1)
    arrays, args = {}, []
    for name in _INS:
        a = _np.ascontiguousarray(inputs[name])
        arrays[f"in_{name}_dram"] = a
        args.append(nc.dram_tensor(f"in_{name}_dram", a.shape, _mybir.dt.from_np(a.dtype), kind="ExternalInput").ap())
    out = nc.dram_tensor("out_dram", inputs["x"].shape, _mybir.dt.float32, kind="ExternalOutput").ap()
    build(nc, *args, out)
    r = _run(nc, [arrays], core_ids=[0])
    return r.results[0]["out_dram"]
```

```python
from contextlib import ExitStack

import concourse.bass as bass
from concourse import mybir
import numpy as np

P = 128
ALU = mybir.AluOpType
ACT = mybir.ActivationFunctionType
AX = mybir.AxisListType
F32 = mybir.dt.float32
BF16 = mybir.dt.bfloat16
I32 = mybir.dt.int32

EPS = 1e-5
FAR = 1.0e30
SKIP = float(1 << 20)
CUTOFF = 5.0


def after(eng, sem, count):
    if not (isinstance(count, int) and count < 1):
        eng.wait_ge(sem, count)


def back(h, par, k, unroll=2):
    return h + (par - k) // unroll, (par - k) % unroll


def build(nc, x, src, dst, attr, weight, ntype, w_qkv, b_qkv, w_ff, b_ff, table, w_dist, b_dist, w_comb, b_comb, out):
    N, D = x.shape
    E, RBF = attr.shape
    SPECIES = table.shape[0]
    DC = D // P
    HD = 32
    HPC = P // HD
    SCALE = float(1.0 / np.sqrt(HD))
    ROWS = 4
    STEP = P * ROWS
    SLOTS = 4
    G = -(-N // STEP)
    REST = N - (G - 1) * STEP
    REST_J = 3
    REST_P = REST // REST_J
    assert REST_P * REST_J == REST and REST_P % 16 == 0 and REST_P <= P and G % 2 == 0
    EB = 2 * P
    B = -(-E // EB)
    T = 2 * B
    FULL_T, REST_E = divmod(E, P)
    assert T == FULL_T + 1 and B % 2 == 1 and T <= P

    ctx = ExitStack()

    def sb(name, shape, dt=F32):
        return ctx.enter_context(nc.sbuf_tensor(name, shape, dt))

    def sem(name):
        return ctx.enter_context(nc.semaphore(name))

    def sems(name):
        return [sem(f"{name}{i}") for i in range(2)]

    ps = ctx.enter_context(nc.psum_tensor("ps", [P, 8, 512], F32))

    def bank(k):
        return ps[:, k, :].rearrange("p (c n) -> p c n", c=2)

    ident = sb("ident", [P, P])
    ones_mean = sb("ones_mean", [P, P])
    head_sum = sb("head_sum", [P, P])
    lane = sb("lane", [P, 1])
    lane_i = sb("lane_i", [P, 1], I32)
    eps_col = sb("eps_col", [P, 1])
    half_pi = sb("half_pi", [P, 1])
    neg_half = sb("neg_half", [P, ROWS])
    wc = sb("wc", [P, 2 * DC, D])
    wc_mean = sb("wc_mean", [P, 2 * DC])
    w_mix = sb("w_mix", [P, DC, D])
    bc = sb("bc", [P, D])
    bc_mean = sb("bc_mean", [P, 1])
    bff_row = sb("bff_row", [P, D])
    bff_col = sb("bff_col", [P, DC])
    bqkv = sb("bqkv", [P, 3 * DC])
    w_raw = sb("w_raw", [P, 3 * DC + DC, D])
    wT = sb("wT", [P, DC, 4 * D])
    wd = sb("wd", [RBF + 1, D])
    tab = sb("tab", [SPECIES, D])
    tab_res = sb("tab_res", [SPECIES, D])
    tab3 = sb("tab3", [SPECIES, 3, D], BF16)
    rows_i = sb("rows_i", [T, 3, P], I32)
    rows_f = sb("rows_f", [T, 4, P])
    cols = sb("cols", [P, 4, T])
    ct = sb("ct", [P, 4, T])
    ct_i = sb("ct_i", [P, T], I32)
    idx = sb("idx", [P, B, 6], I32)
    src_i = sb("src_i", [P, T], I32)
    fcol = sb("fcol", [P, B, 6])
    ty_idx = sb("ty_idx", [P, SLOTS, 1], I32)
    ty = sb("ty", [P, SLOTS, 1], I32)

    xin = sb("xin", [P, SLOTS, ROWS * D])
    zin = sb("zin", [P, 2, ROWS * D])
    zT = sb("zT", [P, 2, DC, ROWS * P])
    stat = sb("stat", [P, 2, ROWS, 6])
    mv = sb("mv", [P, 2, ROWS, 2])
    sd1 = sb("sd1", [P, 2, ROWS])
    r1 = sb("r1", [P, 2, ROWS])
    yn = sb("yn", [P, 2, ROWS * D])
    junk = sb("junk", [P, ROWS, D])
    ss = sb("ss", [P, 2, ROWS])
    sd2 = sb("sd2", [P, 2, ROWS])
    r2 = sb("r2", [P, 2, ROWS])
    on = sb("on", [P, 2, ROWS * D])

    idx_b = sb("idx_b", [P, 3, 6], I32)
    fcol_b = sb("fcol_b", [P, 2, 6])
    xs = sb("xs", [P, 2, 2, D])
    xd = sb("xd", [P, 2, 2, D])
    at = sb("at", [P, 2, 2, RBF])
    atc = sb("atc", [P, 2, RBF + 1])
    dbc = sb("dbc", [P, 2, EB + 1])
    same = sb("same", [P, 2, EB])
    neg = sb("neg", [P, 2, EB])
    hot = sb("hot", [P, EB], BF16)
    xsT = sb("xsT", [P, 2, EB])
    xdT = sb("xdT", [P, 2, 2, EB])
    qT = sb("qT", [P, 2, EB])
    vT = sb("vT", [P, 2, EB])
    prod = sb("prod", [P, 2, EB])
    atT = sb("atT", [RBF + 1, EB])
    emb = sb("emb", [P, 2, EB])
    msg = sb("msg", [P, 2, EB])
    mx = sb("mx", [P, 2, 2, EB + 1])
    dlt = sb("dlt", [P, 2, EB])
    raw = sb("raw", [P, 2, EB])
    ub = sb("ub", [P, 2, EB])
    resc = sb("resc", [P, 2, EB])
    ex = sb("ex", [P, 2, EB])
    ev = sb("ev", [P, 2, EB])
    den = sb("den", [P, 2, 2, EB])
    num = sb("num", [P, 2, 2, EB])
    agg = sb("agg", [P, 2, 2, EB])
    rd = sb("rd", [P, 2, 2, HPC])
    rdx = sb("rdx", [P, 2, 2, P])
    oT = sb("oT", [P, 2, EB])
    zeT = sb("zeT", [P, 2, EB])
    est = sb("est", [P, 2, 6])
    mom = sb("mom", [P, 4, 2])
    er_a = sb("er_a", [P, 4])
    er = sb("er", [P, 4])
    t2 = sb("t2", [P, 2, D])
    ye = sb("ye", [P, 2, 2, D])
    oe = sb("oe", [P, 2, 2, D])

    s_w = sem("weights_landed")
    s_rows = sem("edge_rows_landed")
    s_pad = sem("pads_set")
    s_const = sem("constants_set")
    s_lane = sem("lane_ready")
    s_id = sem("ident_ready")
    s_wchain = sem("weight_arithmetic")
    s_cm = sem("column_mean_ready")
    s_wready = sem("mix_weights_ready")
    s_wtp = sem("weight_transposed")
    s_wtc = sem("weight_copied")
    s_ef = sem("edge_rows_float")
    s_ep = sem("edge_columns_transposed")
    s_ec = sem("edge_columns_copied")
    s_sin = sem("cosine_ready")
    s_echain = sem("edge_arithmetic")
    s_idx = sem("edge_indices_ready")
    s_hs = sem("constants_cleared")
    s_wsum = sem("weight_sums")
    s_tab = sem("table_parts")
    s_pool_passed = sem("pool_waits_passed")
    s_dve_passed = sem("vector_waits_passed")
    n_x = [sem(f"node_rows_landed{i}") for i in range(SLOTS)]
    n_out = sems("node_rows_stored")
    n_ty = [sem(f"type_landed{i}") for i in range(SLOTS)]
    n_ti = sem("type_index_copied")
    n_tf = sem("type_float")
    n_z = sem("node_z_ready")
    n_tp = sem("node_z_transposed")
    n_tc = sem("node_zT_copied")
    n_y = sem("node_product_ready")
    n_st = sem("node_stats")
    n_mv = sem("node_moments")
    n_s1 = sem("node_std1")
    n_r1 = sem("node_rstd1")
    n_yy = sem("node_y_ready")
    n_ss = sem("node_squares_summed")
    n_s2 = sem("node_std2")
    n_r2 = sem("node_rstd2")
    n_oa = sem("node_output_scalar_half")
    n_od = sem("node_output_vector_half")
    e_at = sems("attributes_landed")
    e_g = sems("gathers_landed")
    e_sc = sems("scatter_landed")
    s_w1 = sem("node_weights_landed")
    e_sci = sem("scatter_indices_copied")
    e_idx = sem("block_indices_copied")
    e_fc = sem("block_columns_copied")
    e_atc = sem("attributes_scaled")
    e_bcp = sem("receivers_types_broadcast")
    e_dbc = sem("receivers_copied")
    e_hot = sem("onehot_ready")
    e_same = sem("same_receiver_ready")
    e_neg = sem("restart_offset_ready")
    e_xsp = sem("source_rows_transposed")
    e_xdp = sem("receiver_rows_transposed")
    e_xsc = sem("source_rows_copied")
    e_xdc = sem("receiver_rows_copied")
    e_qp = sem("q_product")
    e_kp = sem("k_product")
    e_vp = sem("v_product")
    e_q = sem("q_ready")
    e_v = sem("v_ready")
    e_prod = sem("qk_ready")
    e_attp = sem("scores_ready")
    e_atp = sem("attributes_transposed")
    e_atT = sem("attributes_copied")
    e_embp = sem("embedding_product")
    e_emb = sem("embedding_copied")
    e_wdp = sem("filter_product")
    e_msg = sem("messages_ready")
    e_m0 = sem("maximum_carried")
    e_m = sem("running_maximum_ready")
    e_d = sem("score_minus_maximum")
    e_raw = sem("rescale_exponential")
    e_u = sem("maximum_drop")
    e_resc = sem("rescale_ready")
    e_ex = sem("exponential_ready")
    e_ev = sem("weighted_values_ready")
    e_den = sem("denominator_ready")
    e_num = sem("numerator_ready")
    e_agg = sem("aggregate_ready")
    e_denp = sem("denominator_columns")
    e_rd = sem("reciprocal_ready")
    e_rdx = sem("reciprocal_spread")
    e_rdp = sem("reciprocal_broadcast")
    e_o = sem("attention_ready")
    e_ffp = sem("ff_product")
    e_z = sem("edge_z_ready")
    e_zp = sem("edge_z_transposed")
    e_st = sem("edge_stats")
    e_mv = sem("edge_moments")
    e_ra = sem("edge_var_eps")
    e_r = sem("edge_rstds")
    e_aggp = sem("aggregate_product")
    e_t2 = sem("aggregate_term_ready")
    e_mixp = sem("mix_product")
    e_y = sem("edge_y_ready")
    e_ss = sem("edge_squares_summed")
    e_oe = sem("edge_output_ready")

    block = ctx.enter_context(nc.Block())

    x_steps = x[0:(G - 1) * STEP, :].rearrange("(g p j) d -> g p (j d)", p=P, j=ROWS)
    o_steps = out[0:(G - 1) * STEP, :].rearrange("(g p j) d -> g p (j d)", p=P, j=ROWS)
    x_rest = x[(G - 1) * STEP:N, :].rearrange("(p j) d -> p (j d)", j=REST_J)
    o_rest = out[(G - 1) * STEP:N, :].rearrange("(p j) d -> p (j d)", j=REST_J)
    attr_blocks = attr[0:(B - 1) * EB, :].rearrange("(b t p) r -> b p t r", t=2, p=P)
    ntype_rows = ntype.rearrange("(n a) -> n a", a=1)

    def cut_to(g_last, np_, nj):
        return (REST_P, REST_J) if g_last else (np_, nj)

    def own(eng, passed):
        eng.sem_inc(passed, 1)

    @block.sync
    def _(sp):
        with nc.allow_non_contiguous_dma(reason="bias columns, once"):
            sp.dma_start(wc[:], w_comb.rearrange("(c p) n -> p c n", p=P)).then_inc(s_w1, 16)
            sp.dma_start(bc[:], b_comb.rearrange("(a n) -> a n", a=1).to_broadcast([P, D])).then_inc(s_w1, 16)
            sp.dma_start(bff_row[:], b_ff.rearrange("(a n) -> a n", a=1).to_broadcast([P, D])).then_inc(s_w1, 16)
            for g in range(SLOTS):
                sp.dma_start(xin[:, g, :], x_steps[g]).then_inc(n_x[g], 16)
            sp.wait_ge(s_pad, 1)
            shifted = dst[1:E]
            for k, a in enumerate((src, dst, shifted)):
                n = a.shape[0]
                full = n // P
                sp.dma_start(rows_i[0:full, k, :], a[0:full * P].rearrange("(t p) -> t p", p=P)).then_inc(s_rows, 16)
                sp.dma_start(rows_i[full:full + 1, k, 0:n - full * P],
                             a[full * P:n].rearrange("(t p) -> t p", t=1)).then_inc(s_rows, 16)
            sp.dma_start(rows_f[0:FULL_T, 3, :], weight[0:FULL_T * P].rearrange("(t p) -> t p", p=P)).then_inc(s_rows, 16)
            sp.dma_start(rows_f[FULL_T:FULL_T + 1, 3, 0:REST_E],
                         weight[FULL_T * P:E].rearrange("(t p) -> t p", t=1)).then_inc(s_rows, 16)
            sp.dma_start(w_raw[:, 0:3 * DC, :], w_qkv.rearrange("(c p) n -> p c n", p=P)).then_inc(s_w, 16)
            sp.dma_start(w_raw[:, 3 * DC:, :], w_ff.rearrange("(c p) n -> p c n", p=P)).then_inc(s_w, 16)
            sp.dma_start(bff_col[:], b_ff.rearrange("(c p) -> p c", p=P)).then_inc(s_w, 16)
            sp.dma_start(bqkv[:], b_qkv.rearrange("(c p) -> p c", p=P)).then_inc(s_w, 16)
            sp.dma_start(wd[0:RBF, :], w_dist).then_inc(s_w, 16)
            sp.dma_start(wd[RBF:RBF + 1, :], b_dist.rearrange("(a n) -> a n", a=1)).then_inc(s_w, 16)
            sp.dma_start(tab[:], table).then_inc(s_w, 16)

        def load(h, q, last=False):
            g = SLOTS * h + q
            sp.wait_ge(n_z, g - SLOTS + 1)
            if last:
                sp.dma_start(xin[0:REST_P, q, 0:REST_J * D], x_rest).then_inc(n_x[q], 16)
            else:
                sp.dma_start(xin[:, q, :], x_steps[g]).then_inc(n_x[q], 16)

        def store(h, q, last=False):
            g = SLOTS * h + q
            sp.wait_ge(n_od, g + 1)
            sp.wait_ge(n_oa, g + 1)
            if last:
                sp.dma_start(o_rest, on[0:REST_P, q % 2, 0:REST_J * D]).then_inc(n_out[q % 2], 16)
            else:
                sp.dma_start(o_steps[g], on[:, q % 2, :]).then_inc(n_out[q % 2], 16)

        H = G // SLOTS
        store_at = lambda h, q, **kw: store(*back(h, q, 3, SLOTS), **kw)
        store(0, 0)
        for q in range(SLOTS):
            load(1, q)
            store_at(1, q)
        with sp.Fori(2, H) as h:
            for q in range(SLOTS):
                load(h, q)
                store_at(h, q)
        for q in range(G % SLOTS):
            load(H, q, last=SLOTS * H + q == G - 1)
            store_at(H, q)
        for g in range(G - 3, G):
            store(g // SLOTS, g % SLOTS, last=g == G - 1)

        def load_attr(h, par):
            after(sp, e_atc, 3 * (2 * h + par - 1))
            sp.dma_start(at[:, par, :, :], attr_blocks[2 * h + par]).then_inc(e_at[par], 16)

        load_attr(0, 0)
        load_attr(0, 1)
        with sp.Fori(1, (B - 1) // 2) as h:
            for par in range(2):
                load_attr(h, par)
        sp.wait_ge(e_atc, 3 * (B - 2))
        e0 = (B - 1) * EB
        sp.dma_start(at[:, 0, 0, :], attr[e0:e0 + P, :]).then_inc(e_at[0], 16)
        sp.dma_start(at[0:REST_E, 0, 1, :], attr[e0 + P:E, :]).then_inc(e_at[0], 16)
        for par in range(2):
            sp.wait_ge(n_out[par], 16 * (G // 2))

    @block.gpsimd
    def _(pool):
        pool.memset(rows_i[:], -1).then_inc(s_const, 1)
        pool.memset(rows_f[:, 3, :], 0.0).then_inc(s_const, 1)
        pool.wait_ge(s_const, 2)
        pool.memset(ident[:], 0.0).then_inc(s_pad, 1)
        pool.memset(neg_half[:], -0.5).then_inc(s_const, 1)
        pool.memset(ones_mean[:], 1.0 / D).then_inc(s_const, 1)
        pool.wait_ge(s_pad, 1)
        pool.affine_select(out=ident[:], in_=ident[:], compare_op=ALU.not_equal, fill=1.0, base=0,
                           pattern=[[-1, P]], channel_multiplier=1).then_inc(s_id, 1)
        pool.wait_ge(s_const, 4)

        def z_add(h, q, np_=P, nj=ROWS):
            g = SLOTS * h + q
            par = q % 2
            pool.wait_ge(n_x[q], 16 * (h + 1))
            after(pool, n_tp, 2 * (g - 1))
            after(pool, n_st, g - 1)
            z = zin[0:np_, par, 0:nj * D].rearrange("p (j d) -> p j d", j=nj)
            xx = xin[0:np_, q, 0:nj * D].rearrange("p (j d) -> p j d", j=nj)
            bb = bff_row[0:np_, :].rearrange("p (a d) -> p a d", a=1).to_broadcast([np_, nj, D])
            pool.tensor_tensor(z, xx, bb, ALU.add).then_inc(n_z, 1)

        def type_gather(h, q):
            g = SLOTS * h + q
            after(pool, n_ty[q], 16 * h)
            own(pool, s_pool_passed)
            pool.tensor_copy(ty_idx[:, q, :], src_i[:, g:g + 1] if isinstance(g, int) else src_i[:, bass.ds(g, 1)]).then_inc(n_ti, 1)
            pool.wait_ge(n_ti, g + 1)
            after(pool, n_tf, g - SLOTS + 1)
            own(pool, s_pool_passed)
            pool.indirect_dma_start(ty[:, q, :], None, ntype_rows, bass.IndirectOffsetOnAxis(ty_idx[:, q, :], 0)).then_inc(n_ty[q], 16)

        def type_float(h, q):
            g = SLOTS * h + q
            pool.wait_ge(n_ty[q], 16 * (h + 1))
            own(pool, s_pool_passed)
            pool.tensor_copy(fcol[:, 2 * h + q // 2, 4 + q % 2:5 + q % 2], ty[:, q, :]).then_inc(n_tf, 1)

        def node(h, q, last=False):
            if last:
                z_add(h, q, REST_P, REST_J)
            else:
                z_add(h, q)
            type_float(*back(h, q, 2, SLOTS))
            type_gather(h, q)

        pool.iota(lane_i[:], [[0, 1]], base=0, channel_multiplier=1).then_inc(s_lane, 1)
        pool.wait_ge(s_w1, 16 * 3)
        z_add(0, 0)
        z_add(0, 1)
        pool.wait_ge(s_idx, 1)
        type_gather(0, 0)
        type_gather(0, 1)
        H = G // SLOTS
        for q in range(2, SLOTS):
            node(0, q)
        for q in range(SLOTS):
            node(1, q)
        with pool.Fori(2, H) as h:
            for q in range(SLOTS):
                node(h, q)
        for q in range(G % SLOTS):
            node(H, q, last=SLOTS * H + q == G - 1)
        for g in range(G - 2, G):
            type_float(g // SLOTS, g % SLOTS)
        pool.wait_ge(n_tf, G)

        def indices(h, par):
            b = 2 * h + par
            after(pool, e_g[par], 64 * h)
            after(pool, e_bcp, b - 1)
            after(pool, e_atc, 3 * (b - 1))
            own(pool, s_pool_passed)
            pool.tensor_copy(idx_b[:, par, :], idx[:, b, :]).then_inc(e_idx, 1)
            pool.tensor_copy(fcol_b[:, par, :], fcol[:, b, :]).then_inc(e_fc, 1)

        def gathers(h, par):
            b = 2 * h + par
            pool.wait_ge(e_idx, b + 1)
            after(pool, e_xsp, b - 1)
            after(pool, e_xdp, b - 1)
            own(pool, s_pool_passed)
            for t in range(2):
                pool.indirect_dma_start(xs[:, par, t, :], None, x, bass.IndirectOffsetOnAxis(idx_b[:, par, t:t + 1], 0)).then_inc(e_g[par], 16)
                pool.indirect_dma_start(xd[:, par, t, :], None, x, bass.IndirectOffsetOnAxis(idx_b[:, par, 2 + t:3 + t], 0)).then_inc(e_g[par], 16)

        def drop(h, par):
            b = 2 * h + par
            pool.wait_ge(e_m, 2 * (b + 1))
            pool.wait_ge(e_m0, b + 1)
            after(pool, e_raw, b)
            pool.tensor_tensor(ub[:], mx[:, par, :, 0:EB], mx[:, par, :, 1:EB + 1], ALU.subtract).then_inc(e_u, 1)

        def weigh(h, par):
            b = 2 * h + par
            pool.wait_ge(e_ex, b + 1)
            pool.wait_ge(e_v, 2 * (b + 1))
            after(pool, e_num, 2 * b)
            pool.tensor_tensor(ev[:], ex[:], vT[:], ALU.mult).then_inc(e_ev, 1)

        def rstds(h, par):
            b = 2 * h + par
            after(pool, e_mv, 2 * (min(b, B) if isinstance(b, int) else b))
            after(pool, e_ss, 2 * (b - 1))
            after(pool, e_y, 2 * (b - 1))
            after(pool, e_oe, 2 * (b - 2))
            own(pool, s_pool_passed)
            pool.tensor_scalar(er_a[:], mom[:, :, 1], 1.0, EPS, ALU.mult, ALU.add).then_inc(e_ra, 1)
            pool.wait_ge(e_ra, b)
            pool.tensor_tensor(er[:], er_a[:], neg_half[:], ALU.pow).then_inc(e_r, 1)

        def scatter_indices(h, par):
            b = 2 * h + par
            own(pool, s_pool_passed)
            pool.tensor_copy(idx_b[:, 2, 2 * par:2 * par + 2], idx[:, b, 4:6]).then_inc(e_sci, 1)

        def scatter(h, par):
            b = 2 * h + par
            pool.wait_ge(e_sci, b + 1)
            pool.wait_ge(e_oe, 2 * (b + 1))
            own(pool, s_pool_passed)
            for t in range(2):
                pool.indirect_dma_start(out, bass.IndirectOffsetOnAxis(idx_b[:, 2, 2 * par + t:2 * par + t + 1], 0), oe[:, par, t, :], None,
                                        bounds_check=N - 1, oob_is_err=False).then_inc(e_sc[par], 16)

        def edge(h, par, now=True, ahead=True, one=True, two=True):
            hn, pn = back(h, par, -1)
            h2, p2 = back(h, par, 2)
            if ahead:
                indices(hn, pn)
                gathers(hn, pn)
            if now:
                drop(h, par)
            if one or two:
                rstds(h, par)
            if two:
                after(pool, e_sc[p2], 16 * 2 * h2)
                own(pool, s_pool_passed)
                scatter_indices(h2, p2)
            if now:
                weigh(h, par)
            if two:
                scatter(h2, p2)

        indices(0, 0)
        gathers(0, 0)
        for par in range(2):
            pool.wait_ge(n_out[par], 16 * (G // 2))
        edge(0, 0, one=False, two=False)
        edge(0, 1, two=False)
        for par in range(2):
            edge(1, par)
        with pool.Fori(2, (B - 1) // 2) as h:
            for par in range(2):
                edge(h, par)
        L = (B - 1) // 2
        edge(L, 0, ahead=False)
        edge(L, 1, now=False, ahead=False)
        edge(L + 1, 0, now=False, ahead=False, one=False)
        pool.wait_ge(e_sc[0], 16 * 2 * (L + 1))
        pool.wait_ge(e_sc[1], 16 * 2 * L)

    @block.tensor
    def _(pe):
        mm = pe.matmul
        pe.wait_ge(s_id, 1)
        pe.wait_ge(s_w, 16 * 7)
        for k in range(DC):
            for r in range(4 * DC):
                pe.transpose(ps[:, 4 + 2 * k + r // 4, (r % 4) * P:(r % 4 + 1) * P],
                             w_raw[:, r, k * P:(k + 1) * P], ident[:]).then_inc(s_wtp, 1)
        pe.wait_ge(s_wchain, 7)
        for k in range(DC):
            last = mm(ps[:, 0, 0:D], ones_mean[:], wc[:, k, :], start=k == 0, stop=k == DC - 1)
        last.then_inc(s_cm, 1)
        pe.wait_ge(s_ef, 1)
        for k in range(4):
            last = pe.transpose(ps[:, 1, k * T:(k + 1) * T], rows_f[:, k, :], ident[0:T, 0:T])
        last.then_inc(s_ep, 1)

        def z_transposes(h, par, np_=P, nj=ROWS):
            g = 2 * h + par
            pe.wait_ge(n_z, g + 1)
            for c in range(DC):
                after(pe, n_tc, 2 * (g - 1))
                for j in range(nj):
                    last = pe.transpose(ps[:, 2 * par + c, j * P:j * P + np_],
                                        zin[0:np_, par, j * D + c * P:j * D + (c + 1) * P], ident[0:np_, 0:np_])
                last.then_inc(n_tp, 1)

        def z_product(h, par, np_=P, nj=ROWS):
            g = 2 * h + par
            pe.wait_ge(n_tc, 2 * (g + 1))
            after(pe, n_yy, g - 1)
            for j in range(nj):
                for k in range(DC):
                    last = mm(ps[0:np_, 4 + 2 * par + j // 2, (j % 2) * D:(j % 2 + 1) * D],
                              zT[:, par, k, j * P:j * P + np_], w_mix[:, k, :], start=k == 0, stop=k == DC - 1)
                if j % 2 == 1 or j == nj - 1:
                    last.then_inc(n_y, 1)

        pe.wait_ge(s_ec, 1)
        pe.wait_ge(s_wtc, 4)
        pe.wait_ge(s_wready, 2)
        z_transposes(0, 0)
        z_transposes(0, 1)
        z_product(0, 0)

        def node(h, par, last=False):
            hn, pn = back(h, par, -1)
            if last:
                z_transposes(hn, pn, REST_P, REST_J)
            else:
                z_transposes(hn, pn)
            z_product(h, par)

        node(0, 1)
        for par in range(2):
            node(1, par)
        with pe.Fori(2, G // 2 - 1) as h:
            for par in range(2):
                node(h, par)
        node(G // 2 - 1, 0, last=True)
        z_product(G // 2 - 1, 1, REST_P, REST_J)

        def project(out_bank, weights, moving, done):
            for c in range(2):
                for k in range(DC):
                    last = mm(bank(out_bank)[:, c, :], wT[:, k, weights + c * P:weights + (c + 1) * P], moving[:, k, :],
                              start=k == 0, stop=k == DC - 1)
            last.then_inc(done, 1)

        def edge(h, par, now=True, one=True):
            b = 2 * h + par
            h1, p1 = back(h, par, 1)
            b1 = 2 * h1 + p1
            if now:
                pe.wait_ge(e_fc, b + 1)
                after(pe, e_st, b - 1)
                for t in range(2):
                    pe.transpose(ps[:, 0, t * P:(t + 1) * P], fcol_b[:, par, 2 + t:3 + t].to_broadcast([P, P]), ident[:])
                for t in range(2):
                    last = pe.transpose(ps[:, 0, EB + t * P:EB + (t + 1) * P], fcol_b[:, par, 4 + t:5 + t].to_broadcast([P, P]), ident[:])
                last.then_inc(e_bcp, 1)
                pe.wait_ge(e_g[par], 64 * (h + 1))
                after(pe, e_z, 2 * (b - 1))
                for c in range(DC):
                    for t in range(2):
                        last = pe.transpose(bank(1)[:, c, t * P:(t + 1) * P], xs[:, par, t, c * P:(c + 1) * P], ident[:])
                last.then_inc(e_xsp, 1)
                after(pe, e_emb, b)
                for c in range(DC):
                    for t in range(2):
                        last = pe.transpose(bank(2)[:, c, t * P:(t + 1) * P], xd[:, par, t, c * P:(c + 1) * P], ident[:])
                last.then_inc(e_xdp, 1)
            if one:
                pe.wait_ge(e_den, 2 * (b1 + 1))
                after(pe, e_rd, b1)
                for t in range(2):
                    for c in range(DC):
                        o = (2 * t + c) * P
                        last = pe.transpose(ps[:, 7, o:o + P], den[:, p1, c, t * P:(t + 1) * P], ident[:])
                last.then_inc(e_denp, 1)
            if now:
                pe.wait_ge(e_xdc, b + 1)
                after(pe, e_t2, b - 1)
                project(3, 0, xdT[:, par], e_qp)
                pe.wait_ge(e_xsc, b + 1)
                after(pe, e_msg, b)
                project(4, D, xsT, e_kp)
            if one:
                pe.wait_ge(e_rdx, b1 + 1)
                pe.wait_ge(e_d, b1 + 1)
                for c in range(DC):
                    for t in range(2):
                        last = pe.transpose(bank(6)[:, c, t * P:(t + 1) * P],
                                            rdx[:, t, c, :], ident[:])
                last.then_inc(e_rdp, 1)
            if now:
                after(pe, e_y, 2 * (b - 1))
                project(5, 2 * D, xsT, e_vp)
                pe.wait_ge(e_atc, 3 * (b + 1))
                pe.wait_ge(e_dbc, 2 * (b + 1))
                pe.wait_ge(e_hot, b + 1)
                for t in range(2):
                    last = pe.transpose(ps[0:RBF + 1, 0, t * P:(t + 1) * P], atc[:, t, :], ident[:])
                last.then_inc(e_atp, 1)
            if one:
                pe.wait_ge(e_o, b1 + 1)
                if now:
                    pe.wait_ge(e_xsc, b + 1)
                project(1, 3 * D, oT, e_ffp)
            if now:
                pe.wait_ge(e_hot, b + 1)
                pe.wait_ge(e_xdc, b + 1)
                for c in range(2):
                    for s in range(3):
                        last = mm(bank(2)[:, c, :], tab3[:, s, c * P:(c + 1) * P], hot[0:SPECIES, :], start=s == 0, stop=s == 2)
                last.then_inc(e_embp, 1)
                pe.wait_ge(e_prod, 2 * (b + 1))
                if one:
                    pe.wait_ge(e_o, b1 + 1)
                for c in range(2):
                    last = mm(bank(6)[:, c, :], head_sum[:], prod[:, c, :], start=True, stop=True)
                last.then_inc(e_attp, 1)
            if one:
                pe.wait_ge(e_agg, 2 * (b1 + 1))
                if now:
                    pe.wait_ge(e_q, 2 * (b + 1))
                for t in range(2):
                    for k in range(DC):
                        last = mm(bank(3)[:, t, :], agg[:, p1, k, t * P:(t + 1) * P], wc[:, 2 + k, :], start=k == 0, stop=k == DC - 1)
                last.then_inc(e_aggp, 1)
            if now:
                pe.wait_ge(e_atT, b + 1)
                for c in range(2):
                    last = mm(bank(4)[:, c, :], wd[:, c * P:(c + 1) * P], atT[:], start=True, stop=True)
                last.then_inc(e_wdp, 1)
            if one:
                pe.wait_ge(e_z, 2 * (b1 + 1))
                for t in range(2):
                    for c in range(DC):
                        last = pe.transpose(bank(0)[:, t, c * P:(c + 1) * P], zeT[:, c, t * P:(t + 1) * P], ident[:])
                last.then_inc(e_zp, 1)
                if now:
                    pe.wait_ge(e_v, 2 * (b + 1))
                for t in range(2):
                    for k in range(DC):
                        last = mm(bank(5)[:, t, :], zeT[:, k, t * P:(t + 1) * P], w_mix[:, k, :], start=k == 0, stop=k == DC - 1)
                last.then_inc(e_mixp, 1)

        pe.wait_ge(n_yy, G)
        edge(0, 0, one=False)
        edge(0, 1)
        for par in range(2):
            edge(1, par)
        with pe.Fori(2, (B - 1) // 2) as h:
            for par in range(2):
                edge(h, par)
        L = (B - 1) // 2
        edge(L, 0)
        edge(L, 1, now=False)

    @block.scalar
    def _(act):
        for k in range(DC):
            for r in range(2):
                act.wait_ge(s_wtp, 8 * k + 4 * r + 4)
                act.activation(wT[:, k, r * 512:(r + 1) * 512], ps[:, 4 + 2 * k + r, :], ACT.Copy).then_inc(s_wtc, 1)
        act.wait_ge(s_echain, 7)
        act.activation(ct[:, 3, :], ct[:, 2, :], ACT.Sin, bias=half_pi[:], scale=-float(np.pi) / CUTOFF).then_inc(s_sin, 1)

        def zT_copy(h, par):
            g = 2 * h + par
            for c in range(DC):
                act.wait_ge(n_tp, 2 * g + c + 1)
                after(act, n_y, 2 * (g - 1))
                act.activation(zT[:, par, c, :], ps[:, 2 * par + c, :], ACT.Copy).then_inc(n_tc, 1)

        def std1(h, par, np_=P, nj=ROWS):
            g = 2 * h + par
            act.wait_ge(n_mv, g + 1)
            after(act, n_r1, g - 1)
            act.activation(sd1[0:np_, par, 0:nj], mv[0:np_, par, 0:nj, 1], ACT.Sqrt, bias=eps_col[0:np_, :]).then_inc(n_s1, 1)

        def squares(h, par, np_=P, nj=ROWS):
            g = 2 * h + par
            act.wait_ge(n_yy, g + 1)
            after(act, n_s2, g)
            for j in range(nj):
                last = act.activation(junk[0:np_, j, :], yn[0:np_, par, j * D:(j + 1) * D], ACT.Square,
                                      scale=float(D ** -0.5), accum_out=ss[0:np_, par, j:j + 1])
            last.then_inc(n_ss, 1)
            act.wait_ge(n_ss, g + 1)
            after(act, n_r2, g - 1)
            act.activation(sd2[0:np_, par, 0:nj], ss[0:np_, par, 0:nj], ACT.Sqrt, bias=eps_col[0:np_, :]).then_inc(n_s2, 1)

        def final(h, par, np_=P):
            g = 2 * h + par
            act.wait_ge(n_r2, g + 1)
            after(act, n_out[par], 16 * h)
            for j in range(2):
                last = act.activation(on[0:np_, par, j * D:(j + 1) * D], yn[0:np_, par, j * D:(j + 1) * D], ACT.Copy,
                                      scale=r2[0:np_, par, j:j + 1])
            last.then_inc(n_oa, 1)

        zT_copy(0, 0)
        std1(0, 0)
        zT_copy(0, 1)
        std1(0, 1)
        squares(0, 0)

        def node(h, par, last=False):
            hn, pn = back(h, par, -1)
            zT_copy(hn, pn)
            if last:
                std1(hn, pn, REST_P, REST_J)
            else:
                std1(hn, pn)
            final(*back(h, par, 1))
            squares(h, par)

        node(0, 1)
        for par in range(2):
            node(1, par)
        with act.Fori(2, G // 2 - 1) as h:
            for par in range(2):
                node(h, par)
        node(G // 2 - 1, 0, last=True)
        final(G // 2 - 1, 0)
        squares(G // 2 - 1, 1, REST_P, REST_J)
        final(G // 2 - 1, 1, REST_P)

        def edge(h, par, now=True, one=True, two=True, partial=False):
            b = 2 * h + par
            h1, p1 = back(h, par, 1)
            b1 = 2 * h1 + p1
            h2, p2 = back(h, par, 2)
            b2 = 2 * h2 + p2
            if now:
                after(act, e_same, b - 1)
                after(act, e_dbc, 2 * b)
                act.activation(dbc[:, par, 0:1], dbc[:, 1 - par, EB:EB + 1], ACT.Copy).then_inc(e_dbc, 1)
                act.wait_ge(e_bcp, b + 1)
                act.activation(dbc[:, par, 1:EB + 1], ps[:, 0, 0:EB], ACT.Copy).then_inc(e_dbc, 1)
                act.wait_ge(e_at[par], 16 * (h + (2 if partial else 1)))
                act.wait_ge(e_fc, b + 1)
                after(act, e_atp, b)
                for t in range(2):
                    act.activation(atc[:, t, 0:RBF], at[:, par, t, :], ACT.Copy, scale=fcol_b[:, par, t:t + 1]).then_inc(e_atc, 1)
                act.activation(atc[:, :, RBF], fcol_b[:, par, 0:2], ACT.Copy).then_inc(e_atc, 1)
                act.wait_ge(e_xsp, b + 1)
                after(act, e_vp, b)
                act.activation(xsT[:].rearrange("p c n -> p (c n)"), ps[:, 1, :], ACT.Copy).then_inc(e_xsc, 1)
                act.wait_ge(e_xdp, b + 1)
                after(act, e_z, 2 * (b - 1))
                act.activation(xdT[:, par].rearrange("p c n -> p (c n)"), ps[:, 2, :], ACT.Copy).then_inc(e_xdc, 1)
            if one:
                act.wait_ge(e_rd, b1 + 1)
                after(act, e_rdp, b1)
                act.activation(rdx[:].rearrange("p t c (h a) -> p (t c h) a", a=HD),
                               rd[:].rearrange("p t c (h a) -> p (t c h) a", a=1).to_broadcast([P, 4 * HPC, HD]), ACT.Copy).then_inc(e_rdx, 1)
            if now:
                act.wait_ge(e_qp, b + 1)
                after(act, e_prod, 2 * b)
                for c in range(2):
                    act.activation(qT[:, c, :], bank(3)[:, c, :], ACT.Identity, bias=bqkv[:, c:c + 1]).then_inc(e_q, 1)
                act.wait_ge(e_vp, b + 1)
                after(act, e_ev, b)
                for c in range(2):
                    act.activation(vT[:, c, :], bank(5)[:, c, :], ACT.Identity, bias=bqkv[:, 4 + c:5 + c]).then_inc(e_v, 1)
            if two:
                act.wait_ge(e_y, 2 * (b2 + 1))
                after(act, e_ra, b2 + 1)
                after(act, e_ss, 2 * b2)
                for t in range(2):
                    act.activation(junk[:, t, :], ye[:, p2, t, :], ACT.Square, scale=float(D ** -0.5), accum_out=mom[:, 2 + t, 1:2]).then_inc(e_ss, 1)
            if now:
                act.wait_ge(e_atp, b + 1)
                after(act, e_wdp, b)
                act.activation(atT[:], ps[0:RBF + 1, 0, 0:EB], ACT.Copy).then_inc(e_atT, 1)
                act.wait_ge(e_embp, b + 1)
                after(act, e_msg, b)
                act.activation(emb[:].rearrange("p c n -> p (c n)"), ps[:, 2, :], ACT.Copy).then_inc(e_emb, 1)
            if now:
                act.wait_ge(e_u, b + 1)
                after(act, e_resc, b)
                act.activation(raw[:], ub[:], ACT.Exp, scale=SCALE).then_inc(e_raw, 1)
                act.wait_ge(e_d, b + 1)
                after(act, e_ev, b)
                act.activation(ex[:], dlt[:], ACT.Exp, scale=SCALE).then_inc(e_ex, 1)
            if two:
                act.wait_ge(e_r, b2 + 2)
                after(act, e_sc[p2], 32 * h2)
                for t in range(2):
                    act.activation(oe[:, p2, t, :], ye[:, p2, t, :], ACT.Copy, scale=er[:, 2 + t:3 + t]).then_inc(e_oe, 1)

        edge(0, 0, one=False, two=False)
        edge(0, 1, two=False)
        for par in range(2):
            edge(1, par)
        with act.Fori(2, (B - 1) // 2) as h:
            for par in range(2):
                edge(h, par)
        L = (B - 1) // 2
        edge(L, 0, partial=True)
        edge(L, 1, now=False)
        edge(L + 1, 0, now=False, one=False)

    @block.vector
    def _(dve):
        dve.memset(head_sum[:], 0.0).then_inc(s_hs, 1)
        dve.memset(half_pi[:], float(np.pi) / 2).then_inc(s_hs, 1)
        for a in (mx, den, num, agg):
            dve.memset(a[:, 1], 0.0).then_inc(s_hs, 1)
        dve.memset(dbc[:, 1, EB:EB + 1], -5.0).then_inc(s_hs, 1)
        dve.memset(eps_col[:], EPS).then_inc(s_hs, 1)
        dve.memset(mom[:], 1.0).then_inc(s_hs, 1)
        dve.wait_ge(s_hs, 9)
        for q in range(HPC):
            dve.memset(head_sum[q * HD:(q + 1) * HD, q * HD:(q + 1) * HD], 1.0).then_inc(s_hs, 1)

        dve.wait_ge(s_w1, 16 * 3)
        dve.wait_ge(s_id, 1)
        for c in range(DC):
            dve.tensor_tensor(wc[:, c, c * P:(c + 1) * P], wc[:, c, c * P:(c + 1) * P], ident[:], ALU.add).then_inc(s_wchain, 1)
        dve.wait_ge(s_wchain, 2)
        dve.tensor_reduce(wc_mean[:], wc[:], AX.X, ALU.add).then_inc(s_wsum, 1)
        dve.tensor_reduce(bc_mean[:], bc[:], AX.X, ALU.add).then_inc(s_wsum, 1)
        dve.wait_ge(s_wsum, 2)
        dve.tensor_scalar(wc_mean[:], wc_mean[:], 1.0 / D, None, ALU.mult).then_inc(s_wsum, 1)
        dve.tensor_scalar(bc_mean[:], bc_mean[:], 1.0 / D, None, ALU.mult).then_inc(s_wsum, 1)
        dve.wait_ge(s_wsum, 4)
        for c in range(2 * DC):
            dve.tensor_scalar(wc[:, c, :], wc[:, c, :], wc_mean[:, c:c + 1], None, ALU.subtract).then_inc(s_wchain, 1)
        dve.tensor_scalar(bc[:], bc[:], bc_mean[:], None, ALU.subtract).then_inc(s_wchain, 1)
        dve.wait_ge(s_cm, 1)
        for c in range(DC):
            dve.tensor_tensor(w_mix[:, c, :], wc[:, c, :], ps[:, 0, 0:D], ALU.subtract).then_inc(s_wready, 1)

        dve.wait_ge(s_rows, 16 * 8)
        dve.tensor_copy(rows_f[:, 0:3, :], rows_i[:]).then_inc(s_ef, 1)
        dve.wait_ge(s_ep, 1)
        dve.tensor_copy(cols[:].rearrange("p k t -> p (k t)"), ps[:, 1, 0:4 * T]).then_inc(s_ec, 1)
        dve.wait_ge(s_ec, 1)
        dve.scalar_tensor_tensor(out=ct[:, 0, :], in0=cols[:, 3, :], scalar=-1.0, in1=cols[:, 3, :], op0=ALU.mult, op1=ALU.max).then_inc(s_echain, 1)
        dve.wait_ge(s_echain, 1)
        dve.tensor_scalar(ct_i[:], ct[:, 0, :], 0.5 / CUTOFF, None, ALU.mult).then_inc(s_echain, 1)
        dve.wait_ge(s_echain, 2)
        dve.tensor_copy(ct[:, 1, :], ct_i[:]).then_inc(s_echain, 1)
        dve.wait_ge(s_echain, 3)
        dve.scalar_tensor_tensor(out=ct[:, 2, :], in0=ct[:, 1, :], scalar=-2.0 * CUTOFF, in1=ct[:, 0, :], op0=ALU.mult, op1=ALU.add).then_inc(s_echain, 1)
        dve.wait_ge(s_echain, 4)
        dve.scalar_tensor_tensor(out=ct[:, 0, :], in0=ct[:, 2, :], scalar=-1.0, in1=ct[:, 2, :], op0=ALU.mult, op1=ALU.max).then_inc(s_echain, 1)
        dve.wait_ge(s_echain, 5)
        dve.tensor_scalar(ct[:, 1, :], ct[:, 0, :], -1.0, 2.0 * CUTOFF, ALU.mult, ALU.add).then_inc(s_echain, 1)
        dve.wait_ge(s_echain, 6)
        dve.tensor_tensor(ct[:, 2, :], ct[:, 0, :], ct[:, 1, :], ALU.min).then_inc(s_echain, 1)
        dve.wait_ge(s_sin, 1)
        dve.tensor_scalar(ct[:, 0, :], ct[:, 3, :], 0.5, 0.5, ALU.mult, ALU.add).then_inc(s_echain, 1)
        dve.tensor_tensor(ct[:, 1, :], cols[:, 1, :], cols[:, 2, :], ALU.is_equal).then_inc(s_echain, 1)
        dve.wait_ge(s_echain, 9)

        def pairs(a):
            return a.rearrange("p (b t) -> p b t", t=2)

        dve.scalar_tensor_tensor(out=fcol[:, :, 0:2], in0=pairs(cols[:, 3, :]), scalar=CUTOFF, in1=pairs(ct[:, 0, :]), op0=ALU.is_lt, op1=ALU.mult).then_inc(s_echain, 1)
        dve.scalar_tensor_tensor(out=idx[:, :, 4:6], in0=pairs(ct[:, 1, :]), scalar=SKIP, in1=pairs(cols[:, 1, :]), op0=ALU.mult, op1=ALU.add).then_inc(s_echain, 1)
        dve.tensor_copy(fcol[:, :, 2:4], pairs(cols[:, 1, :])).then_inc(s_echain, 1)
        dve.tensor_scalar(src_i[:], cols[:, 0, :], 0.0, None, ALU.max).then_inc(s_echain, 1)
        for k in range(2):
            dve.tensor_scalar(idx[:, :, 2 * k:2 * k + 2], pairs(cols[:, k, :]), 0.0, None, ALU.max).then_inc(s_echain, 1)
        dve.wait_ge(s_echain, 15)
        dve.wait_ge(s_w, 16 * 7)
        dve.tensor_copy(tab3[:, 0, :], tab[:]).then_inc(s_tab, 1)
        dve.wait_ge(s_tab, 1)
        dve.tensor_tensor(tab_res[:], tab[:], tab3[:, 0, :], ALU.subtract).then_inc(s_tab, 1)
        dve.wait_ge(s_tab, 2)
        dve.tensor_copy(tab3[:, 1, :], tab_res[:]).then_inc(s_tab, 1)
        dve.wait_ge(s_tab, 3)
        dve.tensor_tensor(tab[:], tab_res[:], tab3[:, 1, :], ALU.subtract).then_inc(s_tab, 1)
        dve.wait_ge(s_tab, 4)
        dve.tensor_copy(tab3[:, 2, :], tab[:]).then_inc(s_tab, 1)
        dve.wait_ge(s_tab, 5)
        dve.wait_ge(s_lane, 1)
        dve.tensor_copy(lane[:], lane_i[:]).then_inc(s_idx, 1)

        def stats(h, par, np_=P, nj=ROWS):
            g = 2 * h + par
            dve.wait_ge(n_z, g + 1)
            after(dve, n_mv, g - 1)
            for j in range(nj):
                last = dve.bn_stats(stat[0:np_, par, j, :], zin[0:np_, par, j * D:(j + 1) * D])
            last.then_inc(n_st, 1)
            dve.wait_ge(n_st, g + 1)
            after(dve, n_s1, g - 1)
            own(dve, s_dve_passed)
            for j in range(nj):
                last = dve.bn_aggr(mv[0:np_, par, j, :], stat[0:np_, par, j, :])
            last.then_inc(n_mv, 1)

        def rstd1(h, par, np_=P, nj=ROWS):
            g = 2 * h + par
            dve.wait_ge(n_s1, g + 1)
            after(dve, n_yy, g - 1)
            dve.reciprocal(r1[0:np_, par, 0:nj], sd1[0:np_, par, 0:nj]).then_inc(n_r1, 1)

        def rstd2(h, par, np_=P, nj=ROWS):
            g = 2 * h + par
            dve.wait_ge(n_s2, g + 1)
            after(dve, n_od, g - 1)
            after(dve, n_oa, g - 1)
            dve.reciprocal(r2[0:np_, par, 0:nj], sd2[0:np_, par, 0:nj]).then_inc(n_r2, 1)

        def y(h, par, np_=P, nj=ROWS):
            g = 2 * h + par
            dve.wait_ge(n_r1, g + 1)
            after(dve, n_ss, g - 1)
            after(dve, n_od, g - 1)
            after(dve, n_oa, g - 1)
            for j in range(nj):
                if j % 2 == 0:
                    dve.wait_ge(n_y, 2 * g + j // 2 + 1)
                last = dve.scalar_tensor_tensor(out=yn[0:np_, par, j * D:(j + 1) * D],
                                                in0=ps[0:np_, 4 + 2 * par + j // 2, (j % 2) * D:(j % 2 + 1) * D],
                                                scalar=r1[0:np_, par, j:j + 1], in1=bc[0:np_, :], op0=ALU.mult, op1=ALU.add)
            last.then_inc(n_yy, 1)

        def final(h, par, np_=P, nj=ROWS):
            g = 2 * h + par
            dve.wait_ge(n_r2, g + 1)
            dve.wait_ge(n_yy, g + 1)
            after(dve, n_out[par], 16 * h)
            for j in range(2, nj):
                last = dve.tensor_scalar(on[0:np_, par, j * D:(j + 1) * D], yn[0:np_, par, j * D:(j + 1) * D],
                                         r2[0:np_, par, j:j + 1], None, ALU.mult)
            last.then_inc(n_od, 1)

        stats(0, 0)
        rstd1(0, 0)
        stats(0, 1)
        y(0, 0)

        def node(h, par, last=False):
            rstd1(h, par)
            rstd2(*back(h, par, 1))
            hn, pn = back(h, par, -1)
            if last:
                stats(hn, pn, REST_P, REST_J)
            else:
                stats(hn, pn)
            final(*back(h, par, 1))
            y(h, par)

        node(0, 1)
        for par in range(2):
            node(1, par)
        with dve.Fori(2, G // 2 - 1) as h:
            for par in range(2):
                node(h, par)
        node(G // 2 - 1, 0, last=True)
        rstd1(G // 2 - 1, 1, REST_P, REST_J)
        rstd2(G // 2 - 1, 0)
        final(G // 2 - 1, 0)
        y(G // 2 - 1, 1, REST_P, REST_J)
        rstd2(G // 2 - 1, 1, REST_P, REST_J)
        final(G // 2 - 1, 1, REST_P, REST_J)

        def edge(h, par, now=True, one=True):
            b = 2 * h + par
            h1, p1 = back(h, par, 1)
            b1 = 2 * h1 + p1
            if now:
                dve.wait_ge(e_bcp, b + 1)
                dve.wait_ge(e_dbc, 2 * (b + 1))
                after(dve, e_embp, b)
                dve.tensor_scalar(hot[0:SPECIES, :], ps[0:SPECIES, 0, EB:2 * EB], lane[0:SPECIES, 0:1], None, ALU.is_equal).then_inc(e_hot, 1)
                dve.tensor_tensor(same[:, par, :], dbc[:, par, 1:EB + 1], dbc[:, par, 0:EB], ALU.is_equal).then_inc(e_same, 1)
                dve.wait_ge(e_same, b + 1)
                dve.tensor_scalar(neg[:, par, :], same[:, par, :], -1.0, FAR, ALU.add, ALU.mult).then_inc(e_neg, 1)
            if one:
                dve.wait_ge(e_denp, b1 + 1)
                after(dve, e_rdx, b1)
                dve.reciprocal(rd[:].rearrange("p t c h -> p (t c h)"), ps[:, 7, :].rearrange("p (a f) -> p a f", f=HD)[:, :, 0]).then_inc(e_rd, 1)
            if now:
                dve.wait_ge(e_kp, b + 1)
                after(dve, e_attp, b)
                for c in range(2):
                    dve.wait_ge(e_q, 2 * b + c + 1)
                    dve.scalar_tensor_tensor(out=prod[:, c, :], in0=bank(4)[:, c, :], scalar=bqkv[:, 2 + c:3 + c], in1=qT[:, c, :],
                                             op0=ALU.add, op1=ALU.mult).then_inc(e_prod, 1)
            if one:
                dve.wait_ge(e_rdp, b1 + 1)
                dve.wait_ge(e_num, 2 * (b1 + 1))
                after(dve, e_ffp, b1)
                dve.tensor_tensor(oT[:], bank(6), num[:, p1], ALU.mult).then_inc(e_o, 1)
                dve.wait_ge(e_ffp, b1 + 1)
                after(dve, e_mixp, b1)
                for c in range(2):
                    dve.scalar_tensor_tensor(out=zeT[:, c, :], in0=bank(1)[:, c, :], scalar=bff_col[:, c:c + 1], in1=xdT[:, p1, c, :],
                                             op0=ALU.add, op1=ALU.add).then_inc(e_z, 1)
            if now:
                after(dve, e_m, 2 * b)
                after(dve, e_u, b - 1)
                dve.tensor_copy(mx[:, par, :, 0:1], mx[:, 1 - par, :, EB:EB + 1]).then_inc(e_m0, 1)
                dve.wait_ge(e_m0, b + 1)
                dve.wait_ge(e_neg, b + 1)
                dve.wait_ge(e_attp, b + 1)
                for c in range(2):
                    dve.tensor_tensor_scan(out=mx[:, par, c, 1:EB + 1], data0=neg[:, par, :], data1=bank(6)[:, c, :],
                                           initial=mx[:, par, c, 0:1], op0=ALU.add, op1=ALU.max).then_inc(e_m, 1)
                dve.wait_ge(e_m, 2 * (b + 1))
                after(dve, e_ex, b)
                dve.tensor_tensor(dlt[:], bank(6), mx[:, par, :, 1:EB + 1], ALU.subtract).then_inc(e_d, 1)
                dve.wait_ge(e_wdp, b + 1)
                dve.wait_ge(e_emb, b + 1)
                dve.tensor_tensor(msg[:], bank(4), emb[:], ALU.mult).then_inc(e_msg, 1)
            if one:
                dve.wait_ge(e_zp, b1 + 1)
                for t in range(2):
                    last = dve.bn_stats(est[:, t, :], bank(0)[:, t, :])
                last.then_inc(e_st, 1)
                dve.wait_ge(e_st, b1 + 1)
                after(dve, e_ra, b1)
                own(dve, s_dve_passed)
                for t in range(2):
                    dve.bn_aggr(mom[:, t, :], est[:, t, :]).then_inc(e_mv, 1)
                dve.wait_ge(e_aggp, b1 + 1)
                after(dve, e_y, 2 * b1)
                dve.tensor_tensor(t2[:], bank(3), bc[:].rearrange("p (a d) -> p a d", a=1).to_broadcast([P, 2, D]), ALU.add).then_inc(e_t2, 1)
            if now:
                dve.wait_ge(e_raw, b + 1)
                after(dve, e_num, 2 * b)
                dve.scalar_tensor_tensor(out=resc[:], in0=raw[:], scalar=1.0,
                                         in1=same[:, par, :].rearrange("p (a n) -> p a n", a=1).to_broadcast([P, 2, EB]),
                                         op0=ALU.min, op1=ALU.mult).then_inc(e_resc, 1)
                dve.wait_ge(e_resc, b + 1)
                dve.wait_ge(e_ex, b + 1)
                after(dve, e_denp, b - 1)
                for c in range(2):
                    after(dve, e_den, 2 * b)
                    dve.tensor_tensor_scan(out=den[:, par, c, :], data0=resc[:, c, :], data1=ex[:, c, :],
                                           initial=den[:, 1 - par, c, EB - 1:EB], op0=ALU.mult, op1=ALU.add).then_inc(e_den, 1)
                dve.wait_ge(e_ev, b + 1)
                after(dve, e_num, 2 * b)
                for c in range(2):
                    dve.tensor_tensor_scan(out=num[:, par, c, :], data0=resc[:, c, :], data1=ev[:, c, :],
                                           initial=num[:, 1 - par, c, EB - 1:EB], op0=ALU.mult, op1=ALU.add).then_inc(e_num, 1)
                dve.wait_ge(e_msg, b + 1)
                after(dve, e_aggp, b - 1)
                after(dve, e_agg, 2 * b)
                for c in range(2):
                    dve.tensor_tensor_scan(out=agg[:, par, c, :], data0=same[:, par, :], data1=msg[:, c, :],
                                           initial=agg[:, 1 - par, c, EB - 1:EB], op0=ALU.mult, op1=ALU.add).then_inc(e_agg, 1)
            if one:
                dve.wait_ge(e_mixp, b1 + 1)
                dve.wait_ge(e_r, b1 + 1)
                dve.wait_ge(e_t2, b1 + 1)
                after(dve, e_oe, 2 * (b1 - 1))
                for t in range(2):
                    dve.scalar_tensor_tensor(out=ye[:, p1, t, :], in0=bank(5)[:, t, :], scalar=er[:, t:t + 1], in1=t2[:, t, :],
                                             op0=ALU.mult, op1=ALU.add).then_inc(e_y, 1)

        edge(0, 0, one=False)
        edge(0, 1)
        for par in range(2):
            edge(1, par)
        with dve.Fori(2, (B - 1) // 2) as h:
            for par in range(2):
                edge(h, par)
        L = (B - 1) // 2
        edge(L, 0)
        edge(L, 1, now=False)

    ctx.close()


_INS = ["x", "src", "dst", "edge_attr_64", "edge_weight", "node_type_100", "L0_gnn_W_qkv", "L0_gnn_b_qkv", "L0_gnn_W_ff",
        "L0_gnn_b_ff", "L1_gnn_embed_table", "L1_gnn_W_dist", "L1_gnn_b_dist", "L1_gnn_W_comb", "L1_gnn_b_comb"]


def kernel(**inputs):
    import numpy as _np
    import concourse.bacc as _bacc
    from concourse import mybir as _mybir
    from concourse.bass_utils import run_bass_kernel_spmd as _run

    nc = _bacc.Bacc("TRN2", target_bir_lowering=False, num_devices=1)
    arrays, args = {}, []
    for name in _INS:
        a = _np.ascontiguousarray(inputs[name])
        arrays[f"in_{name}_dram"] = a
        args.append(nc.dram_tensor(f"in_{name}_dram", a.shape, _mybir.dt.from_np(a.dtype), kind="ExternalInput").ap())
    out = nc.dram_tensor("out_dram", inputs["x"].shape, _mybir.dt.float32, kind="ExternalOutput").ap()
    build(nc, *args, out)
    r = _run(nc, [arrays], core_ids=[0])
    return r.results[0]["out_dram"]
```

```python
from contextlib import ExitStack

import concourse.bass as bass
from concourse import mybir
import numpy as np

P = 128
ALU = mybir.AluOpType
ACT = mybir.ActivationFunctionType
AX = mybir.AxisListType
F32 = mybir.dt.float32
BF16 = mybir.dt.bfloat16
I32 = mybir.dt.int32
F32R = mybir.dt.float32r

EPS = 1e-5
FAR = 1.0e30
SKIP = float(1 << 20)
CUTOFF = 5.0


def after(eng, sem, count):
    if not (isinstance(count, int) and count < 1):
        eng.wait_ge(sem, count)


def back(h, par, k, unroll=2):
    return h + (par - k) // unroll, (par - k) % unroll


def build(nc, x, src, dst, attr, weight, ntype, w_qkv, b_qkv, w_ff, b_ff, table, w_dist, b_dist, w_comb, b_comb, out):
    N, D = x.shape
    E, RBF = attr.shape
    SPECIES = table.shape[0]
    DC = D // P
    HD = 32
    HPC = P // HD
    SCALE = float(1.0 / np.sqrt(HD))
    ROWS = 4
    STEP = P * ROWS
    SLOTS = 4
    G = -(-N // STEP)
    REST = N - (G - 1) * STEP
    REST_J = 3
    REST_P = REST // REST_J
    assert REST_P * REST_J == REST and REST_P % 16 == 0 and REST_P <= P and G % 2 == 0
    EB = 2 * P
    B = -(-E // EB)
    T = 2 * B
    FULL_T, REST_E = divmod(E, P)
    CHUNKS = 10
    CHUNK = E // CHUNKS
    assert CHUNK * CHUNKS == E
    assert T == FULL_T + 1 and B % 2 == 1 and T <= P

    ctx = ExitStack()

    def sb(name, shape, dt=F32):
        return ctx.enter_context(nc.sbuf_tensor(name, shape, dt))

    def sem(name):
        return ctx.enter_context(nc.semaphore(name))

    def sems(name):
        return [sem(f"{name}{i}") for i in range(2)]

    ps = ctx.enter_context(nc.psum_tensor("ps", [P, 8, 512], F32))

    def bank(k):
        return ps[:, k, :].rearrange("p (c n) -> p c n", c=2)

    ident = sb("ident", [P, P])
    ones_mean = sb("ones_mean", [P, P])
    head_sum = sb("head_sum", [P, P])
    lane = sb("lane", [P, 1])
    lane_i = sb("lane_i", [P, 1], I32)
    eps_col = sb("eps_col", [P, 1])
    one_col = sb("one_col", [P, 1])
    far_col = sb("far_col", [P, 1])
    unsorted = sb("unsorted", [1, 1], I32)
    half_pi = sb("half_pi", [P, 1])
    neg_half = sb("neg_half", [P, ROWS])
    wc = sb("wc", [P, 2 * DC, D])
    wc_mean = sb("wc_mean", [P, 2 * DC])
    w_mix = sb("w_mix", [P, DC, D])
    bc = sb("bc", [P, D])
    bc_mean = sb("bc_mean", [P, 1])
    bff_row = sb("bff_row", [P, D])
    bff_col = sb("bff_col", [P, DC])
    bqkv = sb("bqkv", [P, 3 * DC])
    w_raw = sb("w_raw", [P, 3 * DC + DC, D])
    wff = sb("wff", [P, DC, D])
    wd = sb("wd", [RBF + 1, D])
    tab = sb("tab", [SPECIES, D])
    tab_res = sb("tab_res", [SPECIES, D])
    tab3 = sb("tab3", [SPECIES, 3, D], BF16)
    rows_i = sb("rows_i", [T, 3, P], I32)
    rows_f = sb("rows_f", [T, 4, P])
    cols = sb("cols", [P, 4, T])
    ct = sb("ct", [P, 4, T])
    ct_i = sb("ct_i", [P, T], I32)
    idx = sb("idx", [P, B, 6], I32)
    src_i = sb("src_i", [P, T], I32)
    cut = sb("cut", [P, B, 2])
    tyf = sb("tyf", [P, T])
    ty_rows = sb("ty_rows", [T, P])
    ty_idx = sb("ty_idx", [P, SLOTS, 1], I32)
    ty = sb("ty", [P, SLOTS, 1], I32)

    late = ExitStack()
    w_hi, w_lo = (late.enter_context(nc.sbuf_tensor(n, [P, DC, 3 * D], F32R)) for n in ("w_hi", "w_lo"))
    xs_lo, xd_hi = (late.enter_context(nc.sbuf_tensor(n, [P, 2, EB], F32R)) for n in ("xs_lo", "xd_hi"))
    mix_hi, mix_lo, wagg_hi, wagg_lo = (late.enter_context(nc.sbuf_tensor(n, [P, DC, D], F32R))
                                        for n in ("mix_hi", "mix_lo", "wagg_hi", "wagg_lo"))
    z_hi, z_lo, agg_hi, agg_lo = (late.enter_context(nc.sbuf_tensor(n, [P, 2, EB], F32R))
                                  for n in ("z_hi", "z_lo", "agg_hi", "agg_lo"))
    late.close()
    xin = sb("xin", [P, SLOTS, ROWS * D])
    zin = sb("zin", [P, 2, ROWS * D])
    zT = sb("zT", [P, 2, DC, ROWS * P])
    stat = sb("stat", [P, SLOTS, ROWS, 6])
    mv = sb("mv", [P, SLOTS, ROWS, 2])
    sd1 = sb("sd1", [P, SLOTS, ROWS])
    r1 = sb("r1", [P, SLOTS, ROWS])
    early = ExitStack()
    pairs_i, pairs_gt, descents = (early.enter_context(nc.sbuf_tensor(*a)) for a in (
        ("pairs_i", [T, 2, P], I32), ("pairs_gt", [T, P], F32), ("descents", [T, 1], F32)))
    dst_chunk, place, less, tied, early_tied = (early.enter_context(nc.sbuf_tensor(n, [P, CHUNK], dt)) for n, dt in (
        ("dst_chunk", I32), ("place", F32), ("less", F32), ("tied", F32), ("early_tied", F32)))
    s_dst, s_src, edge_i, rank_i = (early.enter_context(nc.sbuf_tensor(n, [P, T], I32)) for n in ("s_dst", "s_src", "edge_i", "rank_i"))
    s_wgt, dst_f, edge_f, rank = (early.enter_context(nc.sbuf_tensor(n, [P, T], F32)) for n in ("s_wgt", "dst_f", "edge_f", "rank"))
    part = early.enter_context(nc.sbuf_tensor("part", [P, 1], F32))
    m_rank, m_src, m_dst = (early.enter_context(nc.sbuf_tensor(n, [P, 1], I32)) for n in ("m_rank", "m_src", "m_dst"))
    m_wgt = early.enter_context(nc.sbuf_tensor("m_wgt", [P, 1], F32))
    m_attr = early.enter_context(nc.sbuf_tensor("m_attr", [P, RBF], F32))
    early.close()
    yn = sb("yn", [P, SLOTS, ROWS * D])
    junk = sb("junk", [P, ROWS, D])
    ss = sb("ss", [P, SLOTS, ROWS])
    sd2 = sb("sd2", [P, SLOTS, ROWS])
    r2 = sb("r2", [P, SLOTS, ROWS])
    on = sb("on", [P, SLOTS, ROWS * D])

    idx_b = sb("idx_b", [P, 3, 6], I32)
    cut_b = sb("cut_b", [P, 2, 2])
    xs = sb("xs", [P, 2, 2, D])
    xd = sb("xd", [P, 2, 2, D])
    at = sb("at", [P, 2, 2, RBF])
    atc = sb("atc", [P, 2, RBF + 1])
    dwin = sb("dwin", [P, 2, EB + 1], I32)
    tybc = sb("tybc", [P, 2, EB])
    same = sb("same", [P, 2, EB])
    neg = sb("neg", [P, 2, EB])
    hot = sb("hot", [P, EB], BF16)
    xs_hi = sb("xs_hi", [P, 2, EB], F32R)
    xd_lo = sb("xd_lo", [P, 2, EB], F32R)
    xdT = sb("xdT", [P, 2, 2, EB])
    qT = sb("qT", [P, 2, EB])
    vT = sb("vT", [P, 2, EB])
    prod = sb("prod", [P, 2, EB])
    atT = sb("atT", [RBF + 1, EB])
    emb = sb("emb", [P, 2, EB])
    msg = sb("msg", [P, 2, EB])
    mx = sb("mx", [P, 2, 2, EB + 1])
    dlt = sb("dlt", [P, 2, EB])
    raw = sb("raw", [P, 2, EB])
    ub = sb("ub", [P, 2, EB])
    resc = sb("resc", [P, 2, EB])
    ex = sb("ex", [P, 2, EB])
    ev = sb("ev", [P, 2, EB])
    den = sb("den", [P, 2, 2, EB])
    num = sb("num", [P, 2, 2, EB])
    agg = sb("agg", [P, 2, 2, EB])
    rd = sb("rd", [P, 2, 2, HPC])
    rdx = sb("rdx", [P, 2, 2, P])
    oT = sb("oT", [P, 2, EB])
    zeT = sb("zeT", [P, 2, EB])
    est = sb("est", [P, 2, 6])
    mom = sb("mom", [P, 4, 2])
    er_a = sb("er_a", [P, 4])
    er = sb("er", [P, 4])
    t2 = sb("t2", [P, 2, D])
    ye = sb("ye", [P, 2, 2, D])
    oe = sb("oe", [P, 2, 2, D])

    s_w = sem("weights_landed")
    s_rows = sem("edge_rows_landed")
    s_pad = sem("pads_set")
    s_const = sem("constants_set")
    s_lane = sem("lane_ready")
    s_id = sem("ident_ready")
    s_wchain = sem("weight_arithmetic")
    s_cm = sem("column_mean_ready")
    s_wready = sem("mix_weights_ready")
    s_wtp = sem("weight_transposed")
    s_wtc = sem("weight_copied")
    s_ef = sem("edge_rows_float")
    s_ep = sem("edge_columns_transposed")
    s_ec = sem("edge_columns_copied")
    s_sin = sem("cosine_ready")
    s_echain = sem("edge_arithmetic")
    s_idx = sem("edge_indices_ready")
    s_hs = sem("constants_cleared")
    s_wsum = sem("weight_sums")
    s_tab = sem("table_parts")
    s_pool_passed = sem("pool_waits_passed")
    s_dve_passed = sem("vector_waits_passed")
    s_sp_passed = sem("sync_waits_passed")
    o_rows = sem("receiver_pairs_landed")
    o_gt = sem("receiver_pairs_compared")
    o_desc = sem("descents_counted")
    o_sum = sem("descents_summed")
    o_flag = sem("order_known")
    o_copied = sem("edges_copied")
    o_attr = sem("attributes_in_order")
    o_done = sem("edges_in_order")
    q_iota = sem("sort_counters_ready")
    q_cols = sem("sort_columns_landed")
    q_base = sem("sort_columns_ready")
    q_chunk = sem("sort_chunk_landed")
    q_used = sem("sort_chunk_used")
    q_step = sem("sort_comparisons")
    q_part = sem("sort_partial_counts")
    q_shift = sem("sort_edge_numbers_shifted")
    q_rank = sem("ranks_ready")
    q_col = sem("moved_columns_ready")
    q_attr = sem("moved_attributes_landed")
    q_out = sem("moved_rows_landed")
    n_x = [sem(f"node_rows_landed{i}") for i in range(SLOTS)]
    n_out = [sem(f"node_rows_stored{i}") for i in range(SLOTS)]
    n_ty = [sem(f"type_landed{i}") for i in range(SLOTS)]
    n_ti = sem("type_index_copied")
    n_tf = sem("type_float")
    n_z = sem("node_z_ready")
    n_tp = sem("node_z_transposed")
    n_tc = sem("node_zT_copied")
    n_y = sem("node_product_ready")
    n_st = sem("node_stats")
    n_mv = sem("node_moments")
    n_s1 = sem("node_std1")
    n_r1 = sem("node_rstd1")
    n_yy = sem("node_y_ready")
    n_ss = sem("node_squares_summed")
    n_s2 = sem("node_std2")
    n_r2 = sem("node_rstd2")
    n_oa = sem("node_output_scalar_half")
    n_od = sem("node_output_vector_half")
    e_at = sems("attributes_landed")
    e_g = sems("gathers_landed")
    e_sc = sems("scatter_landed")
    s_w1 = sem("node_weights_landed")
    e_sci = sem("scatter_indices_copied")
    e_idx = sem("block_indices_copied")
    e_fc = sem("block_columns_copied")
    e_atc = sem("attributes_scaled")
    e_dw = sems("receivers_landed")
    e_tb = sems("types_landed")
    s_tyt = sem("types_transposed")
    s_tyc = sem("types_copied")
    s_tys = sem("types_stored")
    e_hot = sem("onehot_ready")
    e_same = sem("same_receiver_ready")
    e_neg = sem("restart_offset_ready")
    e_xsp = sem("source_rows_transposed")
    e_xdp = sem("receiver_rows_transposed")
    e_xsc = sem("source_rows_copied")
    e_xdc = sem("receiver_rows_copied")
    e_xdh = sem("receiver_high_parts")
    e_xdl = sem("receiver_low_parts")
    e_xsl = sem("source_low_parts")
    s_wlo = sem("weight_low_parts")
    e_zh = sem("edge_z_high_part")
    e_zl = sem("edge_z_low_part")
    e_ah = sem("aggregate_high_part")
    e_al = sem("aggregate_low_part")
    e_qp = sem("q_product")
    e_kp = sem("k_product")
    e_vp = sem("v_product")
    e_q = sem("q_ready")
    e_v = sem("v_ready")
    e_prod = sem("qk_ready")
    e_attp = sem("scores_ready")
    e_atp = sem("attributes_transposed")
    e_atT = sem("attributes_copied")
    e_embp = sem("embedding_product")
    e_emb = sem("embedding_copied")
    e_wdp = sem("filter_product")
    e_msg = sem("messages_ready")
    e_m0 = sem("maximum_carried")
    e_m = sem("running_maximum_ready")
    e_d = sem("score_minus_maximum")
    e_raw = sem("rescale_exponential")
    e_u = sem("maximum_drop")
    e_resc = sem("rescale_ready")
    e_ex = sem("exponential_ready")
    e_ev = sem("weighted_values_ready")
    e_den = sem("denominator_ready")
    e_num = sem("numerator_ready")
    e_agg = sem("aggregate_ready")
    e_denp = sem("denominator_columns")
    e_rd = sem("reciprocal_ready")
    e_rdx = sem("reciprocal_spread")
    e_rdp = sem("reciprocal_broadcast")
    e_o = sem("attention_ready")
    e_ffp = sem("ff_product")
    e_z = sem("edge_z_ready")
    e_zp = sem("edge_z_transposed")
    e_st = sem("edge_stats")
    e_mv = sem("edge_moments")
    e_ra = sem("edge_var_eps")
    e_r = sem("edge_rstds")
    e_aggp = sem("aggregate_product")
    e_t2 = sem("aggregate_term_ready")
    e_mixp = sem("mix_product")
    e_y = sem("edge_y_ready")
    e_ss = sem("edge_squares_summed")
    e_oe = sem("edge_output_ready")

    src_o = nc.dram_tensor("src_o", [E], I32).ap()
    dst_o = nc.dram_tensor("dst_o", [E], I32).ap()
    weight_o = nc.dram_tensor("weight_o", [E], F32).ap()
    attr_o = nc.dram_tensor("attr_o", [E, RBF], F32).ap()
    type_rows = nc.dram_tensor("type_rows", [T * P], F32).ap()

    block = ctx.enter_context(nc.Block())

    x_steps = x[0:(G - 1) * STEP, :].rearrange("(g p j) d -> g p (j d)", p=P, j=ROWS)
    o_steps = out[0:(G - 1) * STEP, :].rearrange("(g p j) d -> g p (j d)", p=P, j=ROWS)
    x_rest = x[(G - 1) * STEP:N, :].rearrange("(p j) d -> p (j d)", j=REST_J)
    o_rest = out[(G - 1) * STEP:N, :].rearrange("(p j) d -> p (j d)", j=REST_J)
    attr_blocks = attr_o[0:(B - 1) * EB, :].rearrange("(b t p) r -> b p t r", t=2, p=P)
    ntype_rows = ntype.rearrange("(n a) -> n a", a=1)

    def inside(g):
        return not isinstance(g, int) or 0 <= g < G

    def size(g):
        return (REST_P, REST_J) if isinstance(g, int) and g == G - 1 else (P, ROWS)

    def node_steps(eng, node, first=0):
        for g in range(first, 2 * SLOTS):
            node(*divmod(g, SLOTS))
        H = (G - 3) // SLOTS
        with eng.Fori(2, H) as h:
            for q in range(SLOTS):
                node(h, q)
        for g in range(SLOTS * H, G):
            node(*divmod(g, SLOTS))

    def within(b):
        return not isinstance(b, int) or 0 <= b < B

    def upto(b):
        return min(b, B) if isinstance(b, int) else b

    def edge_turns(eng, edge):
        for b in range(4):
            edge(*divmod(b, 2))
        with eng.Fori(2, B // 2) as h:
            for par in range(2):
                edge(h, par)
        for b in range(B // 2 * 2, B + 3):
            edge(*divmod(b, 2))

    def own(eng, passed):
        eng.sem_inc(passed, 1)

    @block.sync
    def _(sp):
        with nc.allow_non_contiguous_dma(reason="bias columns, once"):
            sp.dma_start(wc[:], w_comb.rearrange("(c p) n -> p c n", p=P)).then_inc(s_w1, 16)
            sp.dma_start(bc[:], b_comb.rearrange("(a n) -> a n", a=1).to_broadcast([P, D])).then_inc(s_w1, 16)
            sp.dma_start(bff_row[:], b_ff.rearrange("(a n) -> a n", a=1).to_broadcast([P, D])).then_inc(s_w1, 16)
            sp.dma_start(bff_col[:], b_ff.rearrange("(c p) -> p c", p=P)).then_inc(s_w1, 16)
            sp.wait_ge(s_pad, 1)
            for k, a in enumerate((dst, dst[1:E])):
                n = a.shape[0]
                full = n // P
                sp.dma_start(pairs_i[0:full, k, :], a[0:full * P].rearrange("(t p) -> t p", p=P)).then_inc(o_rows, 16)
                sp.dma_start(pairs_i[full:full + 1, k, 0:n - full * P],
                             a[full * P:n].rearrange("(t p) -> t p", t=1)).then_inc(o_rows, 16)
            for g in range(SLOTS):
                sp.dma_start(xin[:, g, :], x_steps[g]).then_inc(n_x[g], 16)
            for to, a in ((src_o, src), (dst_o, dst), (weight_o, weight)):
                sp.dma_start(to.rearrange("(a n) -> a n", n=CHUNK // 2), a.rearrange("(a n) -> a n", n=CHUNK // 2)).then_inc(o_copied, 16)
            sp.wait_ge(o_done, 1)
            for k, a in enumerate((src_o, dst_o, dst_o[1:E])):
                n = a.shape[0]
                full = n // P
                sp.dma_start(rows_i[0:full, k, :], a[0:full * P].rearrange("(t p) -> t p", p=P)).then_inc(s_rows, 16)
                sp.dma_start(rows_i[full:full + 1, k, 0:n - full * P],
                             a[full * P:n].rearrange("(t p) -> t p", t=1)).then_inc(s_rows, 16)
            sp.dma_start(rows_f[0:FULL_T, 3, :], weight_o[0:FULL_T * P].rearrange("(t p) -> t p", p=P)).then_inc(s_rows, 16)
            sp.dma_start(rows_f[FULL_T:FULL_T + 1, 3, 0:REST_E],
                         weight_o[FULL_T * P:E].rearrange("(t p) -> t p", t=1)).then_inc(s_rows, 16)
            sp.dma_start(w_raw[:, 0:3 * DC, :], w_qkv.rearrange("(c p) n -> p c n", p=P)).then_inc(s_w, 16)
            sp.dma_start(w_raw[:, 3 * DC:, :], w_ff.rearrange("(c p) n -> p c n", p=P)).then_inc(s_w, 16)
            sp.dma_start(bqkv[:], b_qkv.rearrange("(c p) -> p c", p=P)).then_inc(s_w, 16)
            sp.dma_start(wd[0:RBF, :], w_dist).then_inc(s_w, 16)
            sp.dma_start(wd[RBF:RBF + 1, :], b_dist.rearrange("(a n) -> a n", a=1)).then_inc(s_w, 16)
            sp.dma_start(tab[:], table).then_inc(s_w, 16)
            sp.wait_ge(o_flag, 1)
            with sp.If(sp.value_load(unsorted[0:1, 0:1], min_val=0, max_val=E) < 2):
                sp.dma_start(attr_o, attr).then_inc(o_attr, 16)

        def load(h, q):
            g = SLOTS * h + q
            sp.wait_ge(n_z, g - SLOTS + 1)
            own(sp, s_sp_passed)
            sp.wait_ge(n_tp, 2 * (g - SLOTS + 1))
            if size(g) == (P, ROWS):
                sp.dma_start(xin[:, q, :], x_steps[g]).then_inc(n_x[q], 16)
            else:
                sp.dma_start(xin[0:REST_P, q, 0:REST_J * D], x_rest).then_inc(n_x[q], 16)

        def store(h, q):
            g = SLOTS * h + q
            sp.wait_ge(n_od, g + 1)
            sp.wait_ge(n_oa, g + 1)
            if size(g) == (P, ROWS):
                sp.dma_start(o_steps[g], on[:, q, :]).then_inc(n_out[q], 16)
            else:
                sp.dma_start(o_rest, on[0:REST_P, q, 0:REST_J * D]).then_inc(n_out[q], 16)

        def node(h, q):
            load(h, q)
            hs, qs = back(h, q, LAG, SLOTS)
            if inside(SLOTS * hs + qs):
                store(hs, qs)

        LAG = 6
        node_steps(sp, node, first=SLOTS)
        for g in range(G - LAG, G):
            store(*divmod(g, SLOTS))

        def row(a, lo, hi):
            return a[lo:hi].rearrange("(a n) -> a n", a=1)

        def edge_loads(h, par):
            b = 2 * h + par
            e0 = EB * b
            after(sp, e_same, b - 1)
            last = isinstance(b, int) and b == B - 1
            n = E - e0 if last else EB
            if isinstance(b, int):
                if b == 0:
                    sp.dma_start(dwin[:, 0, 1:EB + 1], row(dst_o, 0, EB).to_broadcast([P, EB])).then_inc(e_dw[0], 16)
                else:
                    sp.dma_start(dwin[:, par, 0:n + 1], row(dst_o, e0 - 1, e0 + n).to_broadcast([P, n + 1])).then_inc(e_dw[par], 16)
            else:
                sp.dma_start(dwin[:, par, :], dst_o[bass.ds(e0 - 1, EB + 1)].rearrange("(a n) -> a n", a=1).to_broadcast([P, EB + 1])).then_inc(e_dw[par], 16)
            after(sp, e_hot, b - 1)
            own(sp, s_sp_passed)
            sp.dma_start(tybc[:, par, :], type_blocks[b:b + 1, :].to_broadcast([P, EB]) if isinstance(b, int)
                         else type_blocks[bass.ds(b, 1), :].to_broadcast([P, EB])).then_inc(e_tb[par], 16)
            after(sp, e_atc, 3 * (b - 1))
            own(sp, s_sp_passed)
            if last:
                sp.dma_start(at[:, par, 0, :], attr_o[e0:e0 + P, :]).then_inc(e_at[par], 16)
                sp.dma_start(at[0:REST_E, par, 1, :], attr_o[e0 + P:E, :]).then_inc(e_at[par], 16)
            else:
                sp.dma_start(at[:, par, :, :], attr_blocks[b]).then_inc(e_at[par], 16)

        type_blocks = type_rows.rearrange("(b n) -> b n", n=EB)
        sp.wait_ge(s_tyc, 1)
        sp.dma_start(type_rows.rearrange("(t p) -> t p", p=P), ty_rows[:]).then_inc(s_tys, 16)
        sp.wait_ge(s_tys, 16)
        sp.wait_ge(o_attr, 16)
        for b in range(4):
            edge_loads(*divmod(b, 2))
        with sp.Fori(2, B // 2) as h:
            for par in range(2):
                edge_loads(h, par)
        edge_loads(B // 2, 0)
        for q in range(SLOTS):
            sp.wait_ge(n_out[q], 16 * len(range(q, G, SLOTS)))

    @block.gpsimd
    def _(pool):
        pool.memset(rows_i[:], -1).then_inc(s_const, 1)
        pool.memset(rows_f[:, 3, :], 0.0).then_inc(s_const, 1)
        pool.memset(pairs_i[:], -1).then_inc(s_const, 1)
        pool.wait_ge(s_const, 3)
        pool.memset(ident[:], 0.0).then_inc(s_pad, 1)
        pool.memset(neg_half[:], -0.5).then_inc(s_const, 1)
        pool.memset(ones_mean[:], 1.0 / D).then_inc(s_const, 1)
        pool.wait_ge(s_pad, 1)
        pool.affine_select(out=ident[:], in_=ident[:], compare_op=ALU.not_equal, fill=1.0, base=0,
                           pattern=[[-1, P]], channel_multiplier=1).then_inc(s_id, 1)
        pool.wait_ge(s_const, 5)

        def move(t, e0):
            own(pool, s_pool_passed)
            for to, a in ((m_rank, rank_i), (m_src, s_src), (m_dst, s_dst), (m_wgt, s_wgt)):
                pool.tensor_copy(to[:], a[:, t:t + 1] if isinstance(t, int) else a[:, bass.ds(t, 1)]).then_inc(q_col, 1)
            pool.dma_start(m_attr[:], attr[e0:e0 + P, :] if isinstance(t, int) else attr[bass.ds(e0, P), :]).then_inc(q_attr, 16)
            pool.wait_ge(q_col, 4 * (t + 1))
            own(pool, s_pool_passed)
            pool.wait_ge(q_attr, 16 * (t + 1))
            own(pool, s_pool_passed)
            for to, a in ((src_o.rearrange("(n a) -> n a", a=1), m_src), (dst_o.rearrange("(n a) -> n a", a=1), m_dst),
                          (weight_o.rearrange("(n a) -> n a", a=1), m_wgt), (attr_o, m_attr)):
                pool.indirect_dma_start(to, bass.IndirectOffsetOnAxis(m_rank[:], 0), a[:], None,
                                        bounds_check=E - 1, oob_is_err=False).then_inc(q_out, 16)
            pool.wait_ge(q_out, 64 * (t + 1))

        pool.wait_ge(o_flag, 1)
        with pool.If(pool.value_load(unsorted[0:1, 0:1], min_val=0, max_val=E) > 1):
            pool.iota(dst_chunk[:], [[1, CHUNK]], base=0, channel_multiplier=0).then_inc(q_iota, 1)
            pool.iota(edge_i[:, 0:T - 1], [[P, T - 1]], base=0, channel_multiplier=1).then_inc(q_iota, 1)
            pool.iota(edge_i[:, T - 1:T], [[0, 1]], base=E - P, channel_multiplier=1).then_inc(q_iota, 1)
            with nc.allow_non_contiguous_dma(reason="only where the receivers aren't in order"):
                for to, a in ((s_dst, dst), (s_src, src), (s_wgt, weight)):
                    pool.dma_start(to[:, 0:T - 1], a[0:(T - 1) * P].rearrange("(t p) -> p t", p=P)).then_inc(q_cols, 16)
                    pool.dma_start(to[:, T - 1:T], a[E - P:E].rearrange("(p a) -> p a", a=1)).then_inc(q_cols, 16)
            pool.wait_ge(q_base, 4)
            pool.dma_start(dst_chunk[:], dst[0:CHUNK].rearrange("(a n) -> a n", a=1).to_broadcast([P, CHUNK])).then_inc(q_chunk, 16)
            with pool.Fori(1, CHUNKS) as c:
                pool.wait_ge(q_used, c)
                own(pool, s_pool_passed)
                pool.dma_start(dst_chunk[:], dst[bass.ds(c * CHUNK, CHUNK)].rearrange("(a n) -> a n", a=1).to_broadcast([P, CHUNK])).then_inc(q_chunk, 16)
            pool.wait_ge(q_rank, 1)
            pool.wait_ge(o_copied, 16 * 3)
            with pool.Fori(0, T - 1) as t:
                move(t, t * P)
            move(T - 1, E - P)
            pool.sem_inc(o_attr, 16)
        pool.wait_ge(o_copied, 16 * 3)
        pool.sem_inc(o_done, 1)

        def z_add(h, q):
            g = SLOTS * h + q
            np_, nj = size(g)
            pool.wait_ge(n_x[q], 16 * (h + 1))
            after(pool, n_st, g - 1)
            z = zin[0:np_, q % 2, 0:nj * D].rearrange("p (j d) -> p j d", j=nj)
            xx = xin[0:np_, q, 0:nj * D].rearrange("p (j d) -> p j d", j=nj)
            bb = bff_row[0:np_, :].rearrange("p (a d) -> p a d", a=1).to_broadcast([np_, nj, D])
            pool.tensor_tensor(z, xx, bb, ALU.add).then_inc(n_z, 1)

        def type_gather(h, q):
            g = SLOTS * h + q
            after(pool, n_ty[q], 16 * h)
            own(pool, s_pool_passed)
            pool.tensor_copy(ty_idx[:, q, :], src_i[:, g:g + 1] if isinstance(g, int) else src_i[:, bass.ds(g, 1)]).then_inc(n_ti, 1)
            pool.wait_ge(n_ti, g + 1)
            after(pool, n_tf, g - SLOTS + 1)
            own(pool, s_pool_passed)
            pool.indirect_dma_start(ty[:, q, :], None, ntype_rows, bass.IndirectOffsetOnAxis(ty_idx[:, q, :], 0)).then_inc(n_ty[q], 16)

        def type_float(h, q):
            g = SLOTS * h + q
            pool.wait_ge(n_ty[q], 16 * (h + 1))
            own(pool, s_pool_passed)
            pool.tensor_copy(tyf[:, g:g + 1] if isinstance(g, int) else tyf[:, bass.ds(g, 1)], ty[:, q, :]).then_inc(n_tf, 1)

        def node(h, q):
            z_add(h, q)
            type_float(*back(h, q, 2, SLOTS))
            type_gather(h, q)

        pool.iota(lane_i[:], [[0, 1]], base=0, channel_multiplier=1).then_inc(s_lane, 1)
        pool.wait_ge(s_w1, 16 * 4)
        z_add(0, 0)
        z_add(0, 1)
        pool.wait_ge(s_idx, 1)
        type_gather(0, 0)
        type_gather(0, 1)
        node_steps(pool, node, first=2)
        for g in range(G - 2, G):
            type_float(g // SLOTS, g % SLOTS)
        pool.wait_ge(n_tf, G)

        def indices(h, par):
            b = 2 * h + par
            after(pool, e_g[par], 64 * h)
            after(pool, e_atc, 3 * (b - 1))
            own(pool, s_pool_passed)
            pool.tensor_copy(idx_b[:, par, :], idx[:, b, :]).then_inc(e_idx, 1)
            pool.tensor_copy(cut_b[:, par, :], cut[:, b, :]).then_inc(e_fc, 1)

        def gathers(h, par):
            b = 2 * h + par
            pool.wait_ge(e_idx, b + 1)
            after(pool, e_xsp, b - 1)
            after(pool, e_xdp, b - 1)
            own(pool, s_pool_passed)
            for t in range(2):
                pool.indirect_dma_start(xs[:, par, t, :], None, x, bass.IndirectOffsetOnAxis(idx_b[:, par, t:t + 1], 0)).then_inc(e_g[par], 16)
                pool.indirect_dma_start(xd[:, par, t, :], None, x, bass.IndirectOffsetOnAxis(idx_b[:, par, 2 + t:3 + t], 0)).then_inc(e_g[par], 16)

        def drop(h, par):
            b = 2 * h + par
            pool.wait_ge(e_m, 2 * (b + 1))
            pool.wait_ge(e_m0, b + 1)
            after(pool, e_raw, b)
            pool.tensor_tensor(ub[:], mx[:, par, :, 0:EB], mx[:, par, :, 1:EB + 1], ALU.subtract).then_inc(e_u, 1)

        def weigh(h, par):
            b = 2 * h + par
            pool.wait_ge(e_ex, b + 1)
            pool.wait_ge(e_v, 2 * (b + 1))
            after(pool, e_num, 2 * b)
            pool.tensor_tensor(ev[:], ex[:], vT[:], ALU.mult).then_inc(e_ev, 1)

        def rstds(b):
            after(pool, e_mv, 2 * upto(b - 1))
            after(pool, e_ss, 2 * upto(b - 2))
            after(pool, e_y, 2 * upto(b - 2))
            after(pool, e_oe, 2 * upto(b - 3))
            own(pool, s_pool_passed)
            pool.tensor_scalar(er_a[:], mom[:, :, 1], 1.0, EPS, ALU.mult, ALU.add).then_inc(e_ra, 1)
            pool.wait_ge(e_ra, b - 1)
            pool.tensor_tensor(er[:], er_a[:], neg_half[:], ALU.pow).then_inc(e_r, 1)

        def scatter_indices(h, par):
            b = 2 * h + par
            own(pool, s_pool_passed)
            pool.tensor_copy(idx_b[:, 2, 2 * par:2 * par + 2], idx[:, b, 4:6]).then_inc(e_sci, 1)

        def scatter(h, par):
            b = 2 * h + par
            pool.wait_ge(e_sci, b + 1)
            pool.wait_ge(e_oe, 2 * (b + 1))
            own(pool, s_pool_passed)
            for t in range(2):
                pool.indirect_dma_start(out, bass.IndirectOffsetOnAxis(idx_b[:, 2, 2 * par + t:2 * par + t + 1], 0), oe[:, par, t, :], None,
                                        bounds_check=N - 1, oob_is_err=False).then_inc(e_sc[par], 16)

        def edge(h, par):
            b = 2 * h + par
            h3, p3 = back(h, par, 3)
            if within(b - 2) or within(b - 3):
                rstds(b)
            if within(b + 1):
                indices(*back(h, par, -1))
                gathers(*back(h, par, -1))
            if within(b - 1):
                pool.wait_ge(e_ah, upto(b))
                after(pool, e_aggp, upto(b - 1))
                pool.tensor_tensor(agg_lo[:], agg[:, 1 - par], agg_hi[:], ALU.subtract).then_inc(e_al, 1)
            if within(b):
                drop(h, par)
                weigh(h, par)
            if within(b - 1):
                pool.wait_ge(e_zh, upto(b))
                after(pool, e_mixp, upto(b - 1))
                pool.tensor_tensor(z_lo[:], zeT[:], z_hi[:], ALU.subtract).then_inc(e_zl, 1)
            if within(b - 3):
                if isinstance(b, int) and b == 3:
                    for q in range(SLOTS):
                        pool.wait_ge(n_out[q], 16 * len(range(q, G, SLOTS)))
                after(pool, e_sc[p3], 16 * 2 * h3)
                own(pool, s_pool_passed)
                scatter_indices(h3, p3)
                scatter(h3, p3)

        indices(0, 0)
        gathers(0, 0)
        edge_turns(pool, edge)
        L = B // 2
        pool.wait_ge(e_sc[0], 16 * 2 * (L + 1))
        pool.wait_ge(e_sc[1], 16 * 2 * L)

    @block.tensor
    def _(pe):
        mm = pe.matmul
        pe.wait_ge(s_id, 1)
        pe.wait_ge(s_wchain, 7)
        for k in range(DC):
            last = mm(ps[:, 0, 0:D], ones_mean[:], wc[:, k, :], start=k == 0, stop=k == DC - 1)
        last.then_inc(s_cm, 1)
        pe.wait_ge(o_desc, 1)
        pe.wait_ge(s_hs, 11)
        mm(ps[0:1, 3, 0:1], descents[:], one_col[0:T, :], start=True, stop=True).then_inc(o_sum, 1)
        def x_transposes(h, q):
            g = SLOTS * h + q
            np_, nj = size(g)
            pe.wait_ge(n_x[q], 16 * (h + 1))
            for c in range(DC):
                after(pe, n_tc, 2 * (g - 1))
                for j in range(nj):
                    last = pe.transpose(ps[:, 2 * (q % 2) + c, j * P:j * P + np_],
                                        xin[0:np_, q, j * D + c * P:j * D + (c + 1) * P], ident[0:np_, 0:np_])
                last.then_inc(n_tp, 1)

        def z_product(h, q):
            g = SLOTS * h + q
            np_, nj = size(g)
            pe.wait_ge(n_tc, 2 * (g + 1))
            after(pe, n_yy, 2 * (g - 1))
            for j in range(nj):
                for k in range(DC):
                    last = mm(ps[0:np_, 4 + 2 * (q % 2) + j // 2, (j % 2) * D:(j % 2 + 1) * D],
                              zT[:, q % 2, k, j * P:j * P + np_], w_mix[:, k, :], start=k == 0, stop=k == DC - 1)
                if j % 2 == 1 or j == nj - 1:
                    last.then_inc(n_y, 1)

        def node(h, q):
            hn, qn = back(h, q, -1, SLOTS)
            if inside(SLOTS * hn + qn):
                x_transposes(hn, qn)
            else:
                pe.wait_ge(n_tf, G)
                pe.wait_ge(n_tc, 2 * (G - 1))
                pe.transpose(ps[0:T, 2 * (G % 2), 0:P], tyf[:], ident[:]).then_inc(s_tyt, 1)
            z_product(h, q)

        pe.wait_ge(s_wready, 2)
        x_transposes(0, 0)
        pe.wait_ge(s_ef, 1)
        for k in range(4):
            last = pe.transpose(ps[:, 7, k * T:(k + 1) * T], rows_f[:, k, :], ident[0:T, 0:T])
        last.then_inc(s_ep, 1)
        pe.wait_ge(o_flag, 1)
        pe.wait_ge(s_ec, 1)
        node_steps(pe, node)

        def project(out_bank, weights, hi, lo, done):
            for c in range(2):
                o = weights + c * P
                for k in range(DC):
                    mm(bank(out_bank)[:, c, :], w_hi[:, k, o:o + P], hi[:, k, :], start=k == 0, stop=False)
                    mm(bank(out_bank)[:, c, :], w_hi[:, k, o:o + P], lo[:, k, :], start=False, stop=False)
                    last = mm(bank(out_bank)[:, c, :], w_lo[:, k, o:o + P], hi[:, k, :], start=False, stop=k == DC - 1)
            last.then_inc(done, 1)

        def edge_rows_product(out_bank, hi, lo, w_high, w_low, done):
            for t in range(2):
                e = t * P
                for k in range(DC):
                    mm(bank(out_bank)[:, t, :], hi[:, k, e:e + P], w_high[:, k, :], start=k == 0, stop=False)
                    mm(bank(out_bank)[:, t, :], hi[:, k, e:e + P], w_low[:, k, :], start=False, stop=False)
                    last = mm(bank(out_bank)[:, t, :], lo[:, k, e:e + P], w_high[:, k, :], start=False, stop=k == DC - 1)
            last.then_inc(done, 1)

        def receiver_rows(h, par):
            b = 2 * h + par
            pe.wait_ge(e_g[par], 64 * (h + 1))
            after(pe, e_emb, b)
            for c in range(DC):
                for t in range(2):
                    last = pe.transpose(bank(2)[:, c, t * P:(t + 1) * P], xd[:, par, t, c * P:(c + 1) * P], ident[:])
            last.then_inc(e_xdp, 1)

        def source_rows(h, par):
            b = 2 * h + par
            pe.wait_ge(e_g[par], 64 * (h + 1))
            after(pe, e_z, 2 * (b - 1))
            for c in range(DC):
                for t in range(2):
                    last = pe.transpose(bank(1)[:, c, t * P:(t + 1) * P], xs[:, par, t, c * P:(c + 1) * P], ident[:])
            last.then_inc(e_xsp, 1)

        def edge(h, par):
            b = 2 * h + par
            p1 = 1 - par
            now, one, two = within(b), within(b - 1), within(b - 2)
            if two:
                pe.wait_ge(e_z, 2 * upto(b - 1))
                after(pe, e_atT, upto(b))
                for t in range(2):
                    for c in range(DC):
                        last = pe.transpose(bank(0)[:, t, c * P:(c + 1) * P], zeT[:, c, t * P:(t + 1) * P], ident[:])
                last.then_inc(e_zp, 1)
            if one:
                pe.wait_ge(e_den, 2 * upto(b))
                after(pe, e_o, b - 1)
                for t in range(2):
                    for c in range(DC):
                        o = (2 * t + c) * P
                        last = pe.transpose(ps[:, 7, o:o + P], den[:, p1, c, t * P:(t + 1) * P], ident[:])
                last.then_inc(e_denp, 1)
            if two:
                pe.wait_ge(e_v, 2 * upto(b))
                pe.wait_ge(e_zh, upto(b - 1))
                pe.wait_ge(e_zl, upto(b - 1))
                edge_rows_product(5, z_hi, z_lo, mix_hi, mix_lo, e_mixp)
            if now:
                pe.wait_ge(e_xdc, b + 1)
                after(pe, e_t2, b - 1)
                pe.wait_ge(e_xdh, b + 1)
                pe.wait_ge(e_xdl, b + 1)
                project(3, 0, xd_hi, xd_lo, e_qp)
                pe.wait_ge(e_xsc, b + 1)
                pe.wait_ge(e_xsl, b + 1)
                after(pe, e_msg, b)
                project(4, D, xs_hi, xs_lo, e_kp)
            if one:
                pe.wait_ge(e_rdx, upto(b))
                for c in range(DC):
                    for t in range(2):
                        last = pe.transpose(bank(7)[:, c, t * P:(t + 1) * P], rdx[:, t, c, :], ident[:])
                last.then_inc(e_rdp, 1)
            if now:
                after(pe, e_y, 2 * (b - 1))
                project(5, 2 * D, xs_hi, xs_lo, e_vp)
                pe.wait_ge(e_atc, 3 * (b + 1))
                after(pe, e_st, b - 1)
                for t in range(2):
                    last = pe.transpose(ps[0:RBF + 1, 0, t * P:(t + 1) * P], atc[:, t, :], ident[:])
                last.then_inc(e_atp, 1)
                pe.wait_ge(e_hot, b + 1)
                for c in range(2):
                    for s in range(3):
                        last = mm(bank(2)[:, c, :], tab3[:, s, c * P:(c + 1) * P], hot[0:SPECIES, :], start=s == 0, stop=s == 2)
                last.then_inc(e_embp, 1)
                pe.wait_ge(e_prod, 2 * (b + 1))
                after(pe, e_d, b)
                for c in range(2):
                    last = mm(bank(6)[:, c, :], head_sum[:], prod[:, c, :], start=True, stop=True)
                last.then_inc(e_attp, 1)
            if one:
                pe.wait_ge(e_o, upto(b))
                for c in range(2):
                    for k in range(DC):
                        last = mm(bank(1)[:, c, :], wff[:, k, c * P:(c + 1) * P], oT[:, k, :], start=k == 0, stop=k == DC - 1)
                last.then_inc(e_ffp, 1)
            if within(b + 1):
                receiver_rows(*back(h, par, -1))
            if one:
                pe.wait_ge(e_agg, 2 * upto(b))
                pe.wait_ge(e_q, 2 * upto(b + 1))
                pe.wait_ge(e_ah, upto(b))
                pe.wait_ge(e_al, upto(b))
                edge_rows_product(3, agg_hi, agg_lo, wagg_hi, wagg_lo, e_aggp)
            if within(b + 1):
                source_rows(*back(h, par, -1))
            if now:
                pe.wait_ge(e_atT, b + 1)
                for c in range(2):
                    last = mm(bank(4)[:, c, :], wd[:, c * P:(c + 1) * P], atT[:], start=True, stop=True)
                last.then_inc(e_wdp, 1)

        pe.wait_ge(n_yy, 2 * G)
        pe.wait_ge(s_w, 16 * 6)
        for k in range(DC):
            for r in range(4 * DC):
                pe.transpose(ps[:, 4 + 2 * k + r // 4, (r % 4) * P:(r % 4 + 1) * P],
                             w_raw[:, r, k * P:(k + 1) * P], ident[:]).then_inc(s_wtp, 1)
        pe.wait_ge(s_tyc, 1)
        pe.wait_ge(s_wtc, 8)
        pe.wait_ge(s_wlo, 6)
        receiver_rows(0, 0)
        source_rows(0, 0)
        edge_turns(pe, edge)

    @block.scalar
    def _(act):
        def zT_copy(h, q):
            g = SLOTS * h + q
            for c in range(DC):
                act.wait_ge(n_tp, 2 * g + c + 1)
                after(act, n_y, 2 * (g - 1))
                act.activation(zT[:, q % 2, c, :], ps[:, 2 * (q % 2) + c, :], ACT.Identity, bias=bff_col[:, c:c + 1]).then_inc(n_tc, 1)

        def std1(h, q):
            g = SLOTS * h + q
            np_, nj = size(g)
            act.wait_ge(n_mv, g + 1)
            after(act, n_r1, g - SLOTS + 1)
            act.activation(sd1[0:np_, q, 0:nj], mv[0:np_, q, 0:nj, 1], ACT.Sqrt, bias=eps_col[0:np_, :]).then_inc(n_s1, 1)

        def squares(h, q):
            g = SLOTS * h + q
            np_, nj = size(g)
            after(act, n_s2, g)
            for j in range(nj):
                if j % 2 == 0:
                    act.wait_ge(n_yy, 2 * g + j // 2 + 1)
                last = act.activation(junk[0:np_, j, :], yn[0:np_, q, j * D:(j + 1) * D], ACT.Square,
                                      scale=float(D ** -0.5), accum_out=ss[0:np_, q, j:j + 1])
            last.then_inc(n_ss, 1)
            act.wait_ge(n_ss, g + 1)
            after(act, n_r2, g - SLOTS + 1)
            act.activation(sd2[0:np_, q, 0:nj], ss[0:np_, q, 0:nj], ACT.Sqrt, bias=eps_col[0:np_, :]).then_inc(n_s2, 1)

        def final(h, q):
            g = SLOTS * h + q
            np_, nj = size(g)
            act.wait_ge(n_r2, g + 1)
            after(act, n_out[q], 16 * h)
            for j in range(2):
                last = act.activation(on[0:np_, q, j * D:(j + 1) * D], yn[0:np_, q, j * D:(j + 1) * D], ACT.Copy,
                                      scale=r2[0:np_, q, j:j + 1])
            last.then_inc(n_oa, 1)

        def node(h, q):
            g = SLOTS * h + q
            if inside(g + 1):
                zT_copy(*back(h, q, -1, SLOTS))
                std1(*back(h, q, -1, SLOTS))
            if inside(g - 1):
                final(*back(h, q, 1, SLOTS))
            if not inside(g + 1):
                act.wait_ge(s_tyt, 1)
                act.activation(ty_rows[:], ps[0:T, 2 * (G % 2), 0:P], ACT.Copy).then_inc(s_tyc, 1)
            squares(h, q)

        act.wait_ge(s_w1, 16 * 4)
        zT_copy(0, 0)
        act.wait_ge(s_echain, 7)
        act.activation(ct[:, 3, :], ct[:, 2, :], ACT.Sin, bias=half_pi[:], scale=-float(np.pi) / CUTOFF).then_inc(s_sin, 1)
        std1(0, 0)
        node_steps(act, node)
        final(*divmod(G - 1, SLOTS))

        def edge(h, par):
            b = 2 * h + par
            p2 = par
            h3, p3 = back(h, par, 3)
            last = isinstance(b, int) and b == B - 1
            if within(b):
                act.wait_ge(e_xdp, b + 1)
                after(act, e_z, 2 * (b - 1))
                act.activation(xdT[:, par].rearrange("p c n -> p (c n)"), ps[:, 2, :], ACT.Copy).then_inc(e_xdc, 1)
                after(act, e_qp, b)
                act.activation(xd_hi[:].rearrange("p c n -> p (c n)"), ps[:, 2, :], ACT.Copy).then_inc(e_xdh, 1)
                act.wait_ge(e_xsp, b + 1)
                after(act, e_vp, b)
                act.activation(xs_hi[:].rearrange("p c n -> p (c n)"), ps[:, 1, :], ACT.Copy).then_inc(e_xsc, 1)
                act.wait_ge(e_at[par], 16 * (h + (2 if last else 1)))
                act.wait_ge(e_fc, b + 1)
                after(act, e_atp, b)
                for t in range(2):
                    act.activation(atc[:, t, 0:RBF], at[:, par, t, :], ACT.Copy, scale=cut_b[:, par, t:t + 1]).then_inc(e_atc, 1)
                act.activation(atc[:, :, RBF], cut_b[:, par, 0:2], ACT.Copy).then_inc(e_atc, 1)
            if within(b - 1):
                act.wait_ge(e_rd, upto(b))
                after(act, e_rdp, upto(b - 1))
                act.activation(rdx[:].rearrange("p t c (h a) -> p (t c h) a", a=HD),
                               rd[:].rearrange("p t c (h a) -> p (t c h) a", a=1).to_broadcast([P, 4 * HPC, HD]), ACT.Copy).then_inc(e_rdx, 1)
            if within(b - 3):
                act.wait_ge(e_r, b - 1)
                after(act, e_sc[p3], 32 * h3)
                for t in range(2):
                    act.activation(oe[:, p3, t, :], ye[:, p3, t, :], ACT.Copy, scale=er[:, 2 + t:3 + t]).then_inc(e_oe, 1)
            if within(b - 2):
                act.wait_ge(e_y, 2 * upto(b - 1))
                act.wait_ge(e_ra, b - 1)
                after(act, e_ss, 2 * upto(b - 2))
                for t in range(2):
                    act.activation(junk[:, t, :], ye[:, p2, t, :], ACT.Square, scale=float(D ** -0.5), accum_out=mom[:, 2 + t, 1:2]).then_inc(e_ss, 1)
            if within(b):
                act.wait_ge(e_qp, b + 1)
                after(act, e_prod, 2 * b)
                for c in range(2):
                    act.activation(qT[:, c, :], bank(3)[:, c, :], ACT.Identity, bias=bqkv[:, c:c + 1]).then_inc(e_q, 1)
                act.wait_ge(e_vp, b + 1)
                after(act, e_ev, b)
                for c in range(2):
                    act.activation(vT[:, c, :], bank(5)[:, c, :], ACT.Identity, bias=bqkv[:, 4 + c:5 + c]).then_inc(e_v, 1)
                act.wait_ge(e_same, b + 1)
                after(act, e_m, 2 * (b - 1))
                act.activation(neg[:, par, :], same[:, par, :], ACT.Identity, scale=FAR, bias=far_col[:]).then_inc(e_neg, 1)
            if within(b - 1):
                act.wait_ge(e_agg, 2 * upto(b))
                after(act, e_aggp, upto(b - 1))
                act.activation(agg_hi[:], agg[:, 1 - par], ACT.Copy).then_inc(e_ah, 1)
            if within(b):
                act.wait_ge(e_atp, b + 1)
                after(act, e_wdp, b)
                act.activation(atT[:], ps[0:RBF + 1, 0, 0:EB], ACT.Copy).then_inc(e_atT, 1)
                act.wait_ge(e_embp, b + 1)
                after(act, e_msg, b)
                act.activation(emb[:].rearrange("p c n -> p (c n)"), ps[:, 2, :], ACT.Copy).then_inc(e_emb, 1)
                act.wait_ge(e_d, b + 1)
                after(act, e_ev, b)
                act.activation(ex[:], dlt[:], ACT.Exp, scale=SCALE).then_inc(e_ex, 1)
                act.wait_ge(e_u, b + 1)
                after(act, e_resc, b)
                act.activation(raw[:], ub[:], ACT.Exp, scale=SCALE).then_inc(e_raw, 1)
            if within(b - 1):
                act.wait_ge(e_z, 2 * upto(b))
                after(act, e_mixp, upto(b - 1))
                act.activation(z_hi[:], zeT[:], ACT.Copy).then_inc(e_zh, 1)

        act.wait_ge(n_tp, 2 * G)
        act.wait_ge(n_st, G)
        act.wait_ge(n_y, 2 * G)
        for k in range(DC):
            act.wait_ge(s_wtp, 8 * k + 4)
            act.activation(w_hi[:, k, 0:2 * D], ps[:, 4 + 2 * k, :], ACT.Copy).then_inc(s_wtc, 1)
            act.wait_ge(s_wtp, 8 * k + 8)
            act.activation(w_hi[:, k, 2 * D:3 * D], ps[:, 5 + 2 * k, 0:D], ACT.Copy).then_inc(s_wtc, 1)
            act.activation(wff[:, k, :], ps[:, 5 + 2 * k, D:2 * D], ACT.Copy).then_inc(s_wtc, 1)
        act.activation(mix_hi[:], w_mix[:], ACT.Copy).then_inc(s_wtc, 1)
        act.activation(wagg_hi[:], wc[:, DC:2 * DC, :], ACT.Copy).then_inc(s_wtc, 1)
        edge_turns(act, edge)

    @block.vector
    def _(dve):
        dve.memset(head_sum[:], 0.0).then_inc(s_hs, 1)
        dve.memset(half_pi[:], float(np.pi) / 2).then_inc(s_hs, 1)
        for a in (mx, den, num, agg):
            dve.memset(a[:, 1], 0.0).then_inc(s_hs, 1)
        dve.memset(dwin[:, 0, 0:1], -5).then_inc(s_hs, 1)
        dve.memset(eps_col[:], EPS).then_inc(s_hs, 1)
        dve.memset(one_col[:], 1.0).then_inc(s_hs, 1)
        dve.memset(far_col[:], -FAR).then_inc(s_hs, 1)
        dve.memset(mom[:], 1.0).then_inc(s_hs, 1)
        dve.wait_ge(s_hs, 11)
        for q in range(HPC):
            dve.memset(head_sum[q * HD:(q + 1) * HD, q * HD:(q + 1) * HD], 1.0).then_inc(s_hs, 1)

        dve.wait_ge(s_w1, 16 * 4)
        dve.wait_ge(s_id, 1)
        for c in range(DC):
            dve.tensor_tensor(wc[:, c, c * P:(c + 1) * P], wc[:, c, c * P:(c + 1) * P], ident[:], ALU.add).then_inc(s_wchain, 1)
        dve.wait_ge(s_wchain, 2)
        dve.tensor_reduce(wc_mean[:], wc[:], AX.X, ALU.add).then_inc(s_wsum, 1)
        dve.tensor_reduce(bc_mean[:], bc[:], AX.X, ALU.add).then_inc(s_wsum, 1)
        dve.wait_ge(s_wsum, 2)
        dve.tensor_scalar(wc_mean[:], wc_mean[:], 1.0 / D, None, ALU.mult).then_inc(s_wsum, 1)
        dve.tensor_scalar(bc_mean[:], bc_mean[:], 1.0 / D, None, ALU.mult).then_inc(s_wsum, 1)
        dve.wait_ge(s_wsum, 4)
        for c in range(2 * DC):
            dve.tensor_scalar(wc[:, c, :], wc[:, c, :], wc_mean[:, c:c + 1], None, ALU.subtract).then_inc(s_wchain, 1)
        dve.tensor_scalar(bc[:], bc[:], bc_mean[:], None, ALU.subtract).then_inc(s_wchain, 1)
        dve.wait_ge(o_rows, 16 * 4)
        dve.tensor_tensor(pairs_gt[:], pairs_i[:, 0, :], pairs_i[:, 1, :], ALU.is_gt).then_inc(o_gt, 1)
        dve.wait_ge(o_gt, 1)
        dve.tensor_reduce(descents[:], pairs_gt[:], AX.X, ALU.add).then_inc(o_desc, 1)
        dve.wait_ge(s_cm, 1)
        for c in range(DC):
            dve.tensor_tensor(w_mix[:, c, :], wc[:, c, :], ps[:, 0, 0:D], ALU.subtract).then_inc(s_wready, 1)

        dve.wait_ge(o_sum, 1)
        dve.tensor_copy(unsorted[:], ps[0:1, 3, 0:1]).then_inc(o_flag, 1)
        dve.wait_ge(o_flag, 1)

        def compare(c, t):
            n = 5 * (c * T + t)
            d, e, r = (a[:, bass.ds(t, 1)] for a in (dst_f, edge_f, rank))
            dve.tensor_scalar(less[:], dst_chunk[:], d, None, ALU.is_lt).then_inc(q_step, 1)
            dve.tensor_scalar(tied[:], dst_chunk[:], d, None, ALU.is_equal).then_inc(q_step, 1)
            dve.wait_ge(q_step, n + 2)
            own(dve, s_dve_passed)
            dve.scalar_tensor_tensor(out=early_tied[:], in0=place[:], scalar=e, in1=tied[:], op0=ALU.is_lt, op1=ALU.mult).then_inc(q_step, 1)
            dve.wait_ge(q_step, n + 3)
            own(dve, s_dve_passed)
            dve.tensor_tensor(less[:], less[:], early_tied[:], ALU.add).then_inc(q_step, 1)
            dve.wait_ge(q_step, n + 4)
            own(dve, s_dve_passed)
            dve.tensor_reduce(part[:], less[:], AX.X, ALU.add).then_inc(q_part, 1)
            dve.wait_ge(q_part, c * T + t + 1)
            own(dve, s_dve_passed)
            dve.tensor_tensor(r, r, part[:], ALU.add).then_inc(q_step, 1)
            dve.wait_ge(q_step, n + 5)
            own(dve, s_dve_passed)

        with dve.If(dve.value_load(unsorted[0:1, 0:1], min_val=0, max_val=E) > 1):
            dve.wait_ge(q_iota, 3)
            dve.wait_ge(q_cols, 16 * 6)
            dve.memset(rank[:], 0.0).then_inc(q_base, 1)
            dve.tensor_copy(place[:], dst_chunk[:]).then_inc(q_base, 1)
            dve.tensor_copy(edge_f[:], edge_i[:]).then_inc(q_base, 1)
            dve.tensor_copy(dst_f[:], s_dst[:]).then_inc(q_base, 1)
            dve.wait_ge(q_base, 4)
            with dve.Fori(0, CHUNKS) as c:
                dve.wait_ge(q_chunk, 16 * (c + 1))
                own(dve, s_dve_passed)
                with dve.Fori(0, T) as t:
                    compare(c, t)
                dve.tensor_scalar(edge_f[:], edge_f[:], -float(CHUNK), None, ALU.add).then_inc(q_shift, 1)
                dve.wait_ge(q_shift, c + 1)
                own(dve, s_dve_passed)
                dve.sem_inc(q_used, 1)
            dve.tensor_copy(rank_i[:], rank[:]).then_inc(q_rank, 1)

        dve.wait_ge(s_rows, 16 * 8)
        dve.tensor_copy(rows_f[:, 0:3, :], rows_i[:]).then_inc(s_ef, 1)
        dve.wait_ge(s_ep, 1)
        dve.tensor_copy(cols[:].rearrange("p k t -> p (k t)"), ps[:, 7, 0:4 * T]).then_inc(s_ec, 1)
        dve.wait_ge(s_ec, 1)
        dve.scalar_tensor_tensor(out=ct[:, 0, :], in0=cols[:, 3, :], scalar=-1.0, in1=cols[:, 3, :], op0=ALU.mult, op1=ALU.max).then_inc(s_echain, 1)
        dve.wait_ge(s_echain, 1)
        dve.tensor_scalar(ct_i[:], ct[:, 0, :], 0.5 / CUTOFF, None, ALU.mult).then_inc(s_echain, 1)
        dve.wait_ge(s_echain, 2)
        dve.tensor_copy(ct[:, 1, :], ct_i[:]).then_inc(s_echain, 1)
        dve.wait_ge(s_echain, 3)
        dve.scalar_tensor_tensor(out=ct[:, 2, :], in0=ct[:, 1, :], scalar=-2.0 * CUTOFF, in1=ct[:, 0, :], op0=ALU.mult, op1=ALU.add).then_inc(s_echain, 1)
        dve.wait_ge(s_echain, 4)
        dve.scalar_tensor_tensor(out=ct[:, 0, :], in0=ct[:, 2, :], scalar=-1.0, in1=ct[:, 2, :], op0=ALU.mult, op1=ALU.max).then_inc(s_echain, 1)
        dve.wait_ge(s_echain, 5)
        dve.tensor_scalar(ct[:, 1, :], ct[:, 0, :], -1.0, 2.0 * CUTOFF, ALU.mult, ALU.add).then_inc(s_echain, 1)
        dve.wait_ge(s_echain, 6)
        dve.tensor_tensor(ct[:, 2, :], ct[:, 0, :], ct[:, 1, :], ALU.min).then_inc(s_echain, 1)
        dve.wait_ge(s_sin, 1)
        dve.tensor_scalar(ct[:, 0, :], ct[:, 3, :], 0.5, 0.5, ALU.mult, ALU.add).then_inc(s_echain, 1)
        dve.tensor_tensor(ct[:, 1, :], cols[:, 1, :], cols[:, 2, :], ALU.is_equal).then_inc(s_echain, 1)
        dve.wait_ge(s_echain, 9)

        def pairs(a):
            return a.rearrange("p (b t) -> p b t", t=2)

        dve.scalar_tensor_tensor(out=cut[:], in0=pairs(cols[:, 3, :]), scalar=CUTOFF, in1=pairs(ct[:, 0, :]), op0=ALU.is_lt, op1=ALU.mult).then_inc(s_echain, 1)
        dve.scalar_tensor_tensor(out=idx[:, :, 4:6], in0=pairs(ct[:, 1, :]), scalar=SKIP, in1=pairs(cols[:, 1, :]), op0=ALU.mult, op1=ALU.add).then_inc(s_echain, 1)
        dve.tensor_scalar(src_i[:], cols[:, 0, :], 0.0, None, ALU.max).then_inc(s_echain, 1)
        for k in range(2):
            dve.tensor_scalar(idx[:, :, 2 * k:2 * k + 2], pairs(cols[:, k, :]), 0.0, None, ALU.max).then_inc(s_echain, 1)
        dve.wait_ge(s_echain, 14)
        dve.wait_ge(s_lane, 1)
        dve.tensor_copy(lane[:], lane_i[:]).then_inc(s_idx, 1)

        def stats(h, q):
            g = SLOTS * h + q
            np_, nj = size(g)
            dve.wait_ge(n_z, g + 1)
            after(dve, n_mv, g - SLOTS + 1)
            for j in range(nj):
                last = dve.bn_stats(stat[0:np_, q, j, :], zin[0:np_, q % 2, j * D:(j + 1) * D])
            last.then_inc(n_st, 1)

        def moments(h, q):
            g = SLOTS * h + q
            np_, nj = size(g)
            dve.wait_ge(n_st, g + 1)
            after(dve, n_s1, g - SLOTS + 1)
            own(dve, s_dve_passed)
            for j in range(nj):
                last = dve.bn_aggr(mv[0:np_, q, j, :], stat[0:np_, q, j, :])
            last.then_inc(n_mv, 1)

        def rstd1(h, q):
            g = SLOTS * h + q
            np_, nj = size(g)
            dve.wait_ge(n_s1, g + 1)
            after(dve, n_yy, 2 * (g - SLOTS + 1))
            dve.reciprocal(r1[0:np_, q, 0:nj], sd1[0:np_, q, 0:nj]).then_inc(n_r1, 1)

        def y(h, q):
            g = SLOTS * h + q
            np_, nj = size(g)
            dve.wait_ge(n_r1, g + 1)
            after(dve, n_ss, g - SLOTS + 1)
            after(dve, n_od, g - SLOTS + 1)
            after(dve, n_oa, g - SLOTS + 1)
            for j in range(nj):
                if j % 2 == 0:
                    dve.wait_ge(n_y, 2 * g + j // 2 + 1)
                last = dve.scalar_tensor_tensor(out=yn[0:np_, q, j * D:(j + 1) * D],
                                                in0=ps[0:np_, 4 + 2 * (q % 2) + j // 2, (j % 2) * D:(j % 2 + 1) * D],
                                                scalar=r1[0:np_, q, j:j + 1], in1=bc[0:np_, :], op0=ALU.mult, op1=ALU.add)
                if j % 2 == 1 or j == nj - 1:
                    last.then_inc(n_yy, 1)

        def rstd2(h, q):
            g = SLOTS * h + q
            np_, nj = size(g)
            dve.wait_ge(n_s2, g + 1)
            after(dve, n_od, g - SLOTS + 1)
            after(dve, n_oa, g - SLOTS + 1)
            dve.reciprocal(r2[0:np_, q, 0:nj], sd2[0:np_, q, 0:nj]).then_inc(n_r2, 1)

        def final(h, q):
            g = SLOTS * h + q
            np_, nj = size(g)
            dve.wait_ge(n_r2, g + 1)
            dve.wait_ge(n_yy, 2 * (g + 1))
            after(dve, n_out[q], 16 * h)
            for j in range(2, nj):
                last = dve.tensor_scalar(on[0:np_, q, j * D:(j + 1) * D], yn[0:np_, q, j * D:(j + 1) * D],
                                         r2[0:np_, q, j:j + 1], None, ALU.mult)
            last.then_inc(n_od, 1)

        def node(h, q):
            g = SLOTS * h + q
            y(h, q)
            if inside(g - 1):
                final(*back(h, q, 1, SLOTS))
            if inside(g + 2):
                stats(*back(h, q, -2, SLOTS))
            if inside(g + 1):
                rstd1(*back(h, q, -1, SLOTS))
            if inside(g + 2):
                moments(*back(h, q, -2, SLOTS))
            rstd2(h, q)

        for q in range(2):
            stats(0, q)
            moments(0, q)
        rstd1(0, 0)
        node_steps(dve, node)
        final(*divmod(G - 1, SLOTS))

        def edge(h, par):
            b = 2 * h + par
            p1, p2 = 1 - par, par
            now, one, two = within(b), within(b - 1), within(b - 2)
            if now:
                dve.wait_ge(e_xdc, b + 1)
                dve.wait_ge(e_xdh, b + 1)
                after(dve, e_qp, b)
                dve.tensor_tensor(xd_lo[:], xdT[:, par], xd_hi[:], ALU.subtract).then_inc(e_xdl, 1)
                dve.wait_ge(e_xsc, b + 1)
                after(dve, e_vp, b)
                dve.tensor_tensor(xs_lo[:], bank(1), xs_hi[:], ALU.subtract).then_inc(e_xsl, 1)
            if two:
                dve.wait_ge(e_aggp, upto(b - 1))
                after(dve, e_y, 2 * upto(b - 2))
                dve.tensor_tensor(t2[:], bank(3), bc[:].rearrange("p (a d) -> p a d", a=1).to_broadcast([P, 2, D]), ALU.add).then_inc(e_t2, 1)
                dve.wait_ge(e_zp, upto(b - 1))
                after(dve, e_mv, 2 * upto(b - 2))
                for t in range(2):
                    last = dve.bn_stats(est[:, t, :], bank(0)[:, t, :])
                last.then_inc(e_st, 1)
                dve.wait_ge(e_st, upto(b - 1))
                after(dve, e_ra, b - 2)
                own(dve, s_dve_passed)
                for t in range(2):
                    dve.bn_aggr(mom[:, t, :], est[:, t, :]).then_inc(e_mv, 1)
            if one:
                dve.wait_ge(e_wdp, upto(b))
                dve.wait_ge(e_emb, upto(b))
                after(dve, e_agg, 2 * upto(b - 1))
                dve.tensor_tensor(msg[:], bank(4), emb[:], ALU.mult).then_inc(e_msg, 1)
                dve.wait_ge(e_denp, upto(b))
                after(dve, e_rdx, upto(b - 1))
                dve.reciprocal(rd[:].rearrange("p t c h -> p (t c h)"), ps[:, 7, :].rearrange("p (a f) -> p a f", f=HD)[:, :, 0]).then_inc(e_rd, 1)
                dve.wait_ge(e_ev, upto(b))
                after(dve, e_num, 2 * upto(b - 1))
                for c in range(2):
                    dve.tensor_tensor_scan(out=num[:, p1, c, :], data0=resc[:, c, :], data1=ev[:, c, :],
                                           initial=num[:, 1 - p1, c, EB - 1:EB], op0=ALU.mult, op1=ALU.add).then_inc(e_num, 1)
            if two:
                dve.wait_ge(e_mixp, upto(b - 1))
                dve.wait_ge(e_r, b - 1)
                dve.wait_ge(e_t2, upto(b - 1))
                after(dve, e_oe, 2 * (b - 3))
                for t in range(2):
                    dve.scalar_tensor_tensor(out=ye[:, p2, t, :], in0=bank(5)[:, t, :], scalar=er[:, t:t + 1], in1=t2[:, t, :],
                                             op0=ALU.mult, op1=ALU.add).then_inc(e_y, 1)
            if one:
                dve.wait_ge(e_msg, upto(b))
                after(dve, e_al, upto(b - 2))
                for c in range(2):
                    dve.tensor_tensor_scan(out=agg[:, p1, c, :], data0=same[:, p1, :], data1=msg[:, c, :],
                                           initial=agg[:, 1 - p1, c, EB - 1:EB], op0=ALU.mult, op1=ALU.add).then_inc(e_agg, 1)
            if now:
                dve.wait_ge(e_tb[par], 16 * (h + 1))
                after(dve, e_embp, b)
                dve.tensor_scalar(hot[0:SPECIES, :], tybc[0:SPECIES, par, :], lane[0:SPECIES, 0:1], None, ALU.is_equal).then_inc(e_hot, 1)
                dve.wait_ge(e_dw[par], 16 * (h + 1))
                dve.tensor_tensor(same[:, par, :], dwin[:, par, 1:EB + 1], dwin[:, par, 0:EB], ALU.is_equal).then_inc(e_same, 1)
                dve.wait_ge(e_kp, b + 1)
                after(dve, e_attp, b)
                for c in range(2):
                    dve.wait_ge(e_q, 2 * b + c + 1)
                    dve.scalar_tensor_tensor(out=prod[:, c, :], in0=bank(4)[:, c, :], scalar=bqkv[:, 2 + c:3 + c], in1=qT[:, c, :],
                                             op0=ALU.add, op1=ALU.mult).then_inc(e_prod, 1)
            if one:
                dve.wait_ge(e_rdp, upto(b))
                dve.wait_ge(e_num, 2 * upto(b))
                after(dve, e_ffp, upto(b - 1))
                dve.tensor_tensor(oT[:], bank(7), num[:, p1], ALU.mult).then_inc(e_o, 1)
            if now:
                after(dve, e_m, 2 * b)
                after(dve, e_u, b - 1)
                dve.tensor_copy(mx[:, par, :, 0:1], mx[:, 1 - par, :, EB:EB + 1]).then_inc(e_m0, 1)
                dve.wait_ge(e_m0, b + 1)
                dve.wait_ge(e_neg, b + 1)
                dve.wait_ge(e_attp, b + 1)
                for c in range(2):
                    dve.tensor_tensor_scan(out=mx[:, par, c, 1:EB + 1], data0=neg[:, par, :], data1=bank(6)[:, c, :],
                                           initial=mx[:, par, c, 0:1], op0=ALU.add, op1=ALU.max).then_inc(e_m, 1)
                dve.wait_ge(e_m, 2 * (b + 1))
                after(dve, e_ex, b)
                dve.tensor_tensor(dlt[:], bank(6), mx[:, par, :, 1:EB + 1], ALU.subtract).then_inc(e_d, 1)
            if one:
                dve.wait_ge(e_ffp, upto(b))
                after(dve, e_zl, upto(b - 1))
                after(dve, e_zp, upto(b - 1))
                for c in range(2):
                    dve.scalar_tensor_tensor(out=zeT[:, c, :], in0=bank(1)[:, c, :], scalar=bff_col[:, c:c + 1], in1=xdT[:, p1, c, :],
                                             op0=ALU.add, op1=ALU.add).then_inc(e_z, 1)
            if now:
                dve.wait_ge(e_raw, b + 1)
                after(dve, e_num, 2 * b)
                dve.scalar_tensor_tensor(out=resc[:], in0=raw[:], scalar=1.0,
                                         in1=same[:, par, :].rearrange("p (a n) -> p a n", a=1).to_broadcast([P, 2, EB]),
                                         op0=ALU.min, op1=ALU.mult).then_inc(e_resc, 1)
                dve.wait_ge(e_resc, b + 1)
                dve.wait_ge(e_ex, b + 1)
                after(dve, e_denp, b - 1)
                after(dve, e_den, 2 * b)
                for c in range(2):
                    dve.tensor_tensor_scan(out=den[:, par, c, :], data0=resc[:, c, :], data1=ex[:, c, :],
                                           initial=den[:, 1 - par, c, EB - 1:EB], op0=ALU.mult, op1=ALU.add).then_inc(e_den, 1)

        dve.wait_ge(n_tp, 2 * G)
        dve.wait_ge(n_y, 2 * G)
        for k in range(DC):
            dve.wait_ge(s_wtc, 3 * (k + 1))
            dve.tensor_tensor(w_lo[:, k, 0:2 * D], ps[:, 4 + 2 * k, :], w_hi[:, k, 0:2 * D], ALU.subtract).then_inc(s_wlo, 1)
            dve.tensor_tensor(w_lo[:, k, 2 * D:3 * D], ps[:, 5 + 2 * k, 0:D], w_hi[:, k, 2 * D:3 * D], ALU.subtract).then_inc(s_wlo, 1)
        dve.wait_ge(s_wtc, 8)
        dve.tensor_tensor(mix_lo[:], w_mix[:], mix_hi[:], ALU.subtract).then_inc(s_wlo, 1)
        dve.tensor_tensor(wagg_lo[:], wc[:, DC:2 * DC, :], wagg_hi[:], ALU.subtract).then_inc(s_wlo, 1)
        dve.wait_ge(s_w, 16 * 6)
        dve.tensor_copy(tab3[:, 0, :], tab[:]).then_inc(s_tab, 1)
        dve.wait_ge(s_tab, 1)
        dve.tensor_tensor(tab_res[:], tab[:], tab3[:, 0, :], ALU.subtract).then_inc(s_tab, 1)
        dve.wait_ge(s_tab, 2)
        dve.tensor_copy(tab3[:, 1, :], tab_res[:]).then_inc(s_tab, 1)
        dve.wait_ge(s_tab, 3)
        dve.tensor_tensor(tab[:], tab_res[:], tab3[:, 1, :], ALU.subtract).then_inc(s_tab, 1)
        dve.wait_ge(s_tab, 4)
        dve.tensor_copy(tab3[:, 2, :], tab[:]).then_inc(s_tab, 1)
        dve.wait_ge(s_tab, 5)
        edge_turns(dve, edge)

    ctx.close()


_INS = ["x", "src", "dst", "edge_attr_64", "edge_weight", "node_type_100", "L0_gnn_W_qkv", "L0_gnn_b_qkv", "L0_gnn_W_ff",
        "L0_gnn_b_ff", "L1_gnn_embed_table", "L1_gnn_W_dist", "L1_gnn_b_dist", "L1_gnn_W_comb", "L1_gnn_b_comb"]


def kernel(**inputs):
    import numpy as _np
    import concourse.bacc as _bacc
    from concourse import mybir as _mybir
    from concourse.bass_utils import run_bass_kernel_spmd as _run

    nc = _bacc.Bacc("TRN2", target_bir_lowering=False, num_devices=1)
    arrays, args = {}, []
    for name in _INS:
        a = _np.ascontiguousarray(inputs[name])
        arrays[f"in_{name}_dram"] = a
        args.append(nc.dram_tensor(f"in_{name}_dram", a.shape, _mybir.dt.from_np(a.dtype), kind="ExternalInput").ap())
    out = nc.dram_tensor("out_dram", inputs["x"].shape, _mybir.dt.float32, kind="ExternalOutput").ap()
    build(nc, *args, out)
    r = _run(nc, [arrays], core_ids=[0])
    return r.results[0]["out_dram"]
```
